# Optimizing a Trainium2 kernel written in Bass

```python
import numpy as np
import jax
import jax.numpy as jnp

def _softmax(x, axis=-1):
    return jax.nn.softmax(x, axis=axis)

def _gelu(x):
    return jax.nn.gelu(x, approximate=True)

def _silu(x):
    return jax.nn.silu(x)

def _sigmoid(x):
    return jax.nn.sigmoid(x)

def _layernorm(x, axis=-1, eps=1e-05):
    m = jnp.mean(x, axis=axis, keepdims=True)
    v = jnp.var(x, axis=axis, keepdims=True)
    return (x - m) / jnp.sqrt(v + eps)

def _scatter_add(tgt, idx, src, axis=0):
    return tgt.at[idx].add(src)

def _segment_sum(src, seg, n):
    return jax.ops.segment_sum(src, seg, n)
kernel_name = 'mk_prb_d1_jaxref_r4_43d43f'

def setup_inputs(seed: int=0):
    np.random.seed(seed)
    _w = jnp.asarray

    def _L0_attn_setup():
        import jax, jax.numpy as jnp
        import numpy as np
        DIM = 256
        B, S = (4, 1024)
        key = jax.random.key(seed)
        ks = jax.random.split(key, 7)
        s = 1.0 / np.sqrt(DIM)
        return {'x': jax.random.normal(ks[0], (B, S, DIM), dtype=jnp.float32), 'wq': jax.random.uniform(ks[1], (DIM, DIM), minval=-s, maxval=s, dtype=jnp.float32), 'bq': jax.random.uniform(ks[2], (DIM,), minval=-s, maxval=s, dtype=jnp.float32), 'wk': jax.random.uniform(ks[3], (DIM, DIM), minval=-s, maxval=s, dtype=jnp.float32), 'bk': jax.random.uniform(ks[4], (DIM,), minval=-s, maxval=s, dtype=jnp.float32), 'wv': jax.random.uniform(ks[5], (DIM, DIM), minval=-s, maxval=s, dtype=jnp.float32), 'bv': jax.random.uniform(ks[6], (DIM,), minval=-s, maxval=s, dtype=jnp.float32)}
    _L0_attn_in = _L0_attn_setup()

    def _L0_ffn_setup():
        import jax, jax.numpy as jnp
        import numpy as np
        ALPHA = 1.0
        key = jax.random.key(seed)
        ks = jax.random.split(key, 7)
        B, S, IN, OUT = (8, 2048, 256, 256)
        RANK, DDIM, UDIM = (4, 100, 50)
        return {'hidden_states': jax.random.normal(ks[0], (B, S, IN), dtype=jnp.float32), 'W': jax.random.normal(ks[1], (OUT, IN), dtype=jnp.float32) * 0.02, 'b': jax.random.normal(ks[2], (OUT,), dtype=jnp.float32) * 0.02, 'lora_down': jax.random.normal(ks[3], (RANK, DDIM), dtype=jnp.float32) * 0.1, 'lora_up': jax.random.normal(ks[4], (UDIM, RANK), dtype=jnp.float32) * 0.1, 'down_aux': jax.random.normal(ks[5], (DDIM, IN), dtype=jnp.float32) * 0.03, 'up_aux': jax.random.normal(ks[6], (OUT, UDIM), dtype=jnp.float32) * 0.03}
    _L0_ffn_in = _L0_ffn_setup()
    _d = {'L0_attn_x': _L0_attn_in['x'], 'L0_attn_wq': _L0_attn_in['wq'], 'L0_attn_bq': _L0_attn_in['bq'], 'L0_attn_wk': _L0_attn_in['wk'], 'L0_attn_bk': _L0_attn_in['bk'], 'L0_attn_wv': _L0_attn_in['wv'], 'L0_attn_bv': _L0_attn_in['bv'], 'L0_ffn_W': _L0_ffn_in['W'], 'L0_ffn_b': _L0_ffn_in['b'], 'L0_ffn_lora_down': _L0_ffn_in['lora_down'], 'L0_ffn_lora_up': _L0_ffn_in['lora_up'], 'L0_ffn_down_aux': _L0_ffn_in['down_aux'], 'L0_ffn_up_aux': _L0_ffn_in['up_aux']}
    _x0 = _d['L0_attn_x']
    _d['L0_attn_x'] = jax.random.normal(jax.random.fold_in(jax.random.key(seed), 1), (8, 1024, 256), dtype=_x0.dtype)
    del _x0
    return _d

def reference(L0_attn_x, L0_attn_wq, L0_attn_bq, L0_attn_wk, L0_attn_bk, L0_attn_wv, L0_attn_bv, L0_ffn_W, L0_ffn_b, L0_ffn_lora_down, L0_ffn_lora_up, L0_ffn_down_aux, L0_ffn_up_aux):

    def _L0_attn_ref(x, wq, bq, wk, bk, wv, bv):
        import jax, jax.numpy as jnp
        import numpy as np
        DIM = 256
        B, S = (4, 1024)
        scale = x.shape[-1] ** (-0.5)
        q = x @ wq.T + bq
        k = x @ wk.T + bk
        v = x @ wv.T + bv
        scores = jnp.einsum('bqd,bkd->bqk', q, k) * scale
        attn = jax.nn.softmax(scores, axis=-1)
        return jnp.einsum('bqk,bkd->bqd', attn, v)

    def _L0_ffn_ref(hidden_states, W, b, lora_down, lora_up, down_aux, up_aux):
        import jax, jax.numpy as jnp
        import numpy as np
        ALPHA = 1.0
        lilora_weight = up_aux @ (lora_up @ (lora_down @ down_aux))
        base = jnp.einsum('bsi,oi->bso', hidden_states, W) + b
        delta = jnp.einsum('bsi,oi->bso', hidden_states, lilora_weight)
        return base + ALPHA * delta
    x = L0_attn_x
    xn = _layernorm(x, axis=-1)
    x = x + _L0_attn_ref(xn, L0_attn_wq, L0_attn_bq, L0_attn_wk, L0_attn_bk, L0_attn_wv, L0_attn_bv) + _L0_ffn_ref(xn, L0_ffn_W, L0_ffn_b, L0_ffn_lora_down, L0_ffn_lora_up, L0_ffn_down_aux, L0_ffn_up_aux)
    return x

_drawn_inputs = setup_inputs


def setup_inputs(seed=0):
    import zlib

    import numpy as np

    out = dict(_drawn_inputs(seed))
    spreads = {}
    factors = {'L0_attn_wq': 4.408,
     'L0_attn_bq': 8.0,
     'L0_attn_wk': 4.331,
     'L0_attn_bk': 64.0,
     'L0_ffn_b': 2.923,
     'L0_ffn_lora_down': 2.965,
     'L0_ffn_lora_up': 3.319,
     'L0_ffn_down_aux': 3.093,
     'L0_ffn_up_aux': 3.071,
     'L0_attn_bv': 3.235}
    for name, (base, spread) in spreads.items():
        noise = np.random.default_rng([zlib.crc32(name.encode()), seed]).standard_normal(out[name].shape)
        drawn = base * np.exp(spread * noise) if base else spread * noise
        out[name] = jnp.asarray(drawn.astype(out[name].dtype))
    for name, factor in factors.items():
        out[name] = (out[name] * factor).astype(out[name].dtype)
    return out
```

```python
import concourse.bass as bass
from concourse import mybir
from contextlib import ExitStack


def attention_plus_lora_ffn(
    nc: bass.Bass,
    x: bass.AP,
    wq: bass.AP,
    bq: bass.AP,
    wk: bass.AP,
    bk: bass.AP,
    wv: bass.AP,
    bv: bass.AP,
    ffn_w: bass.AP,
    ffn_b: bass.AP,
    lora_down: bass.AP,
    lora_up: bass.AP,
    down_aux: bass.AP,
    up_aux: bass.AP,
    out: bass.AP,
):
    f32 = mybir.dt.float32
    f32r = mybir.dt.float32r
    ALU = mybir.AluOpType
    ACT = mybir.ActivationFunctionType
    AX = mybir.AxisListType

    B, S, D = x.shape
    PT = 128
    TILES = S // PT
    DT = D // PT
    HALF = S // 2
    HT = TILES // 2
    RANK, DDIM = lora_down.shape
    UDIM = lora_up.shape[0]
    SCALE = float(D) ** -0.5
    EPS = 1e-5
    DMA = 16

    x_v = x.rearrange("b (p n) d -> b p (n d)", n=TILES)
    out_v = out.rearrange("b (p n) d -> b p n d", n=TILES)

    def rows(w):
        return w.rearrange("(t p) n -> p t n", p=PT)

    def column(v):
        return v.rearrange("(t p) -> p t", p=PT)

    def row_for_all(v):
        return v.rearrange("(a n) -> a n", a=1).partition_broadcast(PT).rearrange("p a n -> p (a n)")

    ctx = ExitStack()
    with ctx:
        def sb(name, shape, dt=f32):
            return ctx.enter_context(nc.sbuf_tensor(name, shape, dt))

        def bank(name):
            return ctx.enter_context(nc.psum_tensor(name, [PT, 512], f32))

        def sem(name):
            return ctx.enter_context(nc.semaphore(name))

        wq_sb = sb("wq_sb", [PT, DT, D])
        wk_sb = sb("wk_sb", [PT, DT, D])
        wv_sb = sb("wv_sb", [PT, DT, D])
        ffn_w_sb = sb("ffn_w_sb", [PT, DT, D])
        bq_col = sb("bq_col", [PT, DT])
        bk_col = sb("bk_col", [PT, DT])
        bk_wide = sb("bk_wide", [PT, DT, PT])
        bv_all = sb("bv_all", [PT, D])
        ffn_b_all = sb("ffn_b_all", [PT, D])
        bias_all = sb("bias_all", [PT, D])
        lora_down_t = sb("lora_down_t", [DDIM, RANK])
        lora_up_t = sb("lora_up_t", [RANK, UDIM])
        down_aux_sb = sb("down_aux_sb", [DDIM, D])
        up_aux_pad = sb("up_aux_pad", [PT, DT, PT])
        up_aux_t = sb("up_aux_t", [PT, D])
        low_rank = sb("low_rank", [RANK, D])
        mid_rank = sb("mid_rank", [UDIM, D])
        ffn_w_t = sb("ffn_w_t", [PT, DT, D])
        ffn_full_t = sb("ffn_full_t", [PT, DT, D])
        identity = sb("identity", [PT, PT])
        minus_half = sb("minus_half", [PT, TILES])
        eps_all = sb("eps_all", [PT, TILES])
        a_hi = sb("a_hi", [PT, DT, D], f32r)
        a_lo = sb("a_lo", [PT, DT, D], f32r)
        vf_hi = sb("vf_hi", [PT, DT, 2 * D], f32r)
        vf_lo = sb("vf_lo", [PT, DT, 2 * D], f32r)
        from_bias = sb("from_bias", [PT, D + DT + 1])
        c_row = from_bias[:, 0:D]
        y_bias = from_bias[:, D:D + DT]
        c_const = from_bias[:, D + DT:D + DT + 1]

        x_sb = sb("x_sb", [PT, TILES, D])
        xn = sb("xn", [PT, TILES, D])
        x_bias = sb("x_bias", [PT, TILES, D])
        prod = sb("prod", [PT, TILES, D])
        base = sb("base", [PT, TILES, D])
        stats = sb("stats", [PT, TILES, 6])
        mean_var = sb("mean_var", [PT, TILES, 2])
        var_eps = sb("var_eps", [PT, TILES])
        rstd = sb("rstd", [PT, TILES])
        c_sum = sb("c_sum", [PT, TILES])
        c = sb("c", [PT, TILES])
        xt_hi = sb("xt_hi", [PT, DT, S], f32r)
        xt_lo = sb("xt_lo", [PT, DT, S], f32r)
        yt_hi = sb("yt_hi", [PT, DT, S], f32r)
        yt_lo = sb("yt_lo", [PT, DT, S], f32r)
        v_hl = sb("v_hl", [PT, TILES, 2 * D], f32r)
        p = sb("p", [PT, S])
        pt_hi = sb("pt_hi", [PT, TILES, PT], f32r)
        pt_lo = sb("pt_lo", [PT, TILES, PT], f32r)
        half_max = sb("half_max", [PT, TILES, 2])
        full_max = sb("full_max", [PT, TILES])
        exp_bias = sb("exp_bias", [PT, TILES])
        p_sum = sb("p_sum", [PT, TILES])
        p_sum_inv = sb("p_sum_inv", [PT, TILES])
        with_low = sb("with_low", [PT, 2, D])
        out_sb = sb("out_sb", [PT, TILES, D])

        s_ps = ctx.enter_context(nc.psum_tensor("s_ps", [PT, 2 * 512], f32))
        t_ps = [bank(f"t_ps{h}") for h in range(2)]
        o_ps = [bank(f"o_ps{i}") for i in range(2)]
        g_ps = [bank(f"g_ps{i}") for i in range(2)]

        x0_loaded = [sem(f"x0_loaded{j}") for j in range(4)]
        x_loaded = sem("x_loaded")
        qk_loaded = sem("qk_loaded")
        lora_loaded = sem("lora_loaded")
        vw_loaded = sem("vw_loaded")
        bias_loaded = sem("bias_loaded")
        stored = [sem(f"stored{j}") for j in range(TILES // 2)]
        zeroed = sem("zeroed")
        identity_made = sem("identity_made")
        bk_spread = sem("bk_spread")
        bias_made = sem("bias_made")
        a_mm = sem("a_mm")
        from_bias_mm = sem("from_bias_mm")
        weights_mm = sem("weights_mm")
        low_rank_mm = sem("low_rank_mm")
        mid_rank_mm = sem("mid_rank_mm")
        full_mm = sem("full_mm")
        a_hi_made = sem("a_hi_made")
        a_lo_made = sem("a_lo_made")
        from_bias_made = sem("from_bias_made")
        wv_hi_made = sem("wv_hi_made")
        wv_lo_made = sem("wv_lo_made")
        low_rank_made = sem("low_rank_made")
        up_aux_t_made = sem("up_aux_t_made")
        mid_rank_made = sem("mid_rank_made")
        ffn_w_t_made = sem("ffn_w_t_made")
        ffn_full_made = sem("ffn_full_made")
        ffn_hi_made = sem("ffn_hi_made")
        ffn_lo_made = sem("ffn_lo_made")
        stats_made = sem("stats_made")
        mean_var_made = sem("mean_var_made")
        var_eps_made = sem("var_eps_made")
        rstd_made = sem("rstd_made")
        xn_made = sem("xn_made")
        x_bias_made = sem("x_bias_made")
        prod_made = sem("prod_made")
        c_sum_made = sem("c_sum_made")
        c_made = sem("c_made")
        xt_mm = sem("xt_mm")
        xt_hi_made = sem("xt_hi_made")
        xt_lo_made = sem("xt_lo_made")
        yt_mm = sem("yt_mm")
        yt_hi_made = sem("yt_hi_made")
        yt_lo_made = sem("yt_lo_made")
        vf_mm = sem("vf_mm")
        v_hi_made = sem("v_hi_made")
        v_lo_made = sem("v_lo_made")
        base_made = sem("base_made")
        score_mm = sem("score_mm")
        half_max_made = sem("half_max_made")
        full_max_made = sem("full_max_made")
        exp_bias_made = sem("exp_bias_made")
        p_made = sem("p_made")
        pt_mm = sem("pt_mm")
        pt_hi_made = sem("pt_hi_made")
        pt_lo_made = sem("pt_lo_made")
        pv_mm = sem("pv_mm")
        inv_made = sem("inv_made")
        with_low_made = sem("with_low_made")
        out_made = sem("out_made")

        def wait(eng, semaphore, count):
            if isinstance(count, int) and count <= 0:
                return
            eng.wait_ge(semaphore, count)

        XT_GROUPS = [(h, d) for h in range(2) for d in range(DT)]
        xt_bank = [g_ps[0][:, :], g_ps[1][:, :], s_ps[:, 0:512], s_ps[:, 512:1024]]
        NG = len(XT_GROUPS)

        block = ctx.enter_context(nc.Block())

        @block.sync
        def _(sp):
            for j in range(4):
                n = TILES // 4
                sp.dma_start(x_sb[:, j * n:(j + 1) * n, :],
                             x_v[0, :, j * n * D:(j + 1) * n * D].rearrange("p (n d) -> p n d", d=D))\
                  .then_inc(x0_loaded[j], DMA)

            def load(b):
                sp.wait_ge(xn_made, TILES * b)
                sp.wait_ge(x_bias_made, b)
                sp.dma_start(x_sb[:, :, :], x_v[b, :, :].rearrange("p (n d) -> p n d", d=D))\
                  .then_inc(x_loaded, DMA)

            def store(b, j):
                sp.wait_ge(out_made, TILES * b + 2 * j + 2)
                sp.dma_start(out_v[b, :, 2 * j:2 * j + 2, :], out_sb[:, 2 * j:2 * j + 2, :])\
                  .then_inc(stored[j], DMA)

            load(1)
            with sp.Fori(0, B - 2) as b:
                for j in range(TILES // 2 - 1):
                    store(b, j)
                load(b + 2)
                store(b, TILES // 2 - 1)
            for b in range(B - 2, B):
                for j in range(TILES // 2):
                    store(b, j)
            for j in range(TILES // 2):
                sp.wait_ge(stored[j], DMA * B)

        @block.gpsimd
        def _(pool):
            nc.gpsimd.memset(identity[:, :], 0.0).then_inc(zeroed, 1)
            nc.gpsimd.memset(up_aux_pad[:, :, :], 0.0).then_inc(zeroed, 1)
            nc.gpsimd.memset(minus_half[:, :], -0.5).then_inc(zeroed, 1)
            nc.gpsimd.memset(eps_all[:, :], EPS).then_inc(zeroed, 1)
            pool.wait_ge(zeroed, 1)
            nc.gpsimd.affine_select(out=identity[:, :], in_=identity[:, :], compare_op=ALU.not_equal, fill=1.0,
                                    base=0, pattern=[[-1, PT]], channel_multiplier=1).then_inc(identity_made, 1)
            pool.wait_ge(bias_loaded, 2 * DMA)
            nc.gpsimd.tensor_tensor(bias_all[:, :], bv_all[:, :], ffn_b_all[:, :], ALU.add).then_inc(bias_made, 1)
            pool.wait_ge(bias_made, 1)
            pool.wait_ge(zeroed, 4)

            def make_rstd(b):
                pool.wait_ge(mean_var_made, TILES * (b + 1))
                nc.gpsimd.tensor_tensor(var_eps[:, :], mean_var[:, :, 1], eps_all[:, :], ALU.add)\
                  .then_inc(var_eps_made, 1)
                pool.wait_ge(var_eps_made, b + 1)
                nc.gpsimd.tensor_tensor(rstd[:, :], var_eps[:, :], minus_half[:, :], ALU.pow)\
                  .then_inc(rstd_made, 1)

            def make_x_bias(b):
                wait(pool, base_made, TILES * b)
                nc.gpsimd.tensor_tensor(x_bias[:, :, :], x_sb[:, :, :],
                                        bias_all[:, :].unsqueeze(1).to_broadcast([PT, TILES, D]), ALU.add)\
                  .then_inc(x_bias_made, 1)

            def make_prod(b):
                wait(pool, c_made, b)
                for h in range(2):
                    pool.wait_ge(xn_made, TILES * b + (h + 1) * HT)
                    t = slice(h * HT, (h + 1) * HT)
                    nc.gpsimd.tensor_tensor(prod[:, t, :], xn[:, t, :],
                                            c_row.unsqueeze(1).to_broadcast([PT, HT, D]), ALU.mult)\
                      .then_inc(prod_made, 1)

            for j in range(4):
                pool.wait_ge(x0_loaded[j], DMA)
            make_rstd(0)
            make_x_bias(0)
            pool.wait_ge(from_bias_made, 1)
            make_prod(0)
            with pool.Fori(1, B) as b:
                pool.wait_ge(x_loaded, DMA * b)
                make_x_bias(b)
                make_rstd(b)
                make_prod(b)

        @block.scalar
        def _(act):
            act.dma_start(wq_sb[:, :, :], rows(wq)).then_inc(qk_loaded, DMA)
            act.dma_start(wk_sb[:, :, :], rows(wk)).then_inc(qk_loaded, DMA)
            with nc.allow_non_contiguous_dma(reason="a few hundred words of biases and LoRA factors"):
                act.dma_start(bq_col[:, :], column(bq)).then_inc(qk_loaded, DMA)
                act.dma_start(bk_col[:, :], column(bk)).then_inc(qk_loaded, DMA)
                act.dma_start(lora_down_t[:, :], lora_down.rearrange("r d -> d r")).then_inc(lora_loaded, DMA)
                act.dma_start(lora_up_t[:, :], lora_up.rearrange("u r -> r u")).then_inc(lora_loaded, DMA)
            act.dma_start(down_aux_sb[:, :], down_aux).then_inc(lora_loaded, DMA)
            act.wait_ge(zeroed, 2)
            act.dma_start(up_aux_pad[:, :, 0:UDIM], rows(up_aux)).then_inc(lora_loaded, DMA)
            act.dma_start(wv_sb[:, :, :], rows(wv)).then_inc(vw_loaded, DMA)
            act.dma_start(ffn_w_sb[:, :, :], rows(ffn_w)).then_inc(vw_loaded, DMA)
            act.dma_start(bv_all[:, :], row_for_all(bv)).then_inc(bias_loaded, DMA)
            act.dma_start(ffn_b_all[:, :], row_for_all(ffn_b)).then_inc(bias_loaded, DMA)

            act.wait_ge(a_mm, 1)
            nc.scalar.activation(a_hi[:, :, :], s_ps[:, 0:512].rearrange("p (t n) -> p t n", t=DT),
                                 ACT.Copy, scale=SCALE).then_inc(a_hi_made, 1)
            act.wait_ge(low_rank_mm, 1)
            nc.scalar.activation(low_rank[:, :], o_ps[1][0:RANK, 0:D], ACT.Copy).then_inc(low_rank_made, 1)
            act.wait_ge(mid_rank_mm, 1)
            nc.scalar.activation(mid_rank[:, :], o_ps[1][0:UDIM, D:2 * D], ACT.Copy).then_inc(mid_rank_made, 1)
            act.wait_ge(weights_mm, 1)
            nc.scalar.activation(up_aux_t[:, :], t_ps[1][:, 0:D], ACT.Copy).then_inc(up_aux_t_made, 1)
            act.wait_ge(weights_mm, 2)
            nc.scalar.activation(ffn_w_t[:, :, :], t_ps[0][:, :].rearrange("p (t n) -> p t n", t=DT),
                                 ACT.Copy).then_inc(ffn_w_t_made, 1)
            act.wait_ge(weights_mm, 3)
            nc.scalar.activation(vf_hi[:, :, 0:D], s_ps[:, 512:1024].rearrange("p (t n) -> p t n", t=DT),
                                 ACT.Copy).then_inc(wv_hi_made, 1)
            act.wait_ge(ffn_full_made, 1)
            nc.scalar.activation(vf_hi[:, :, D:2 * D], ffn_full_t[:, :, :], ACT.Copy).then_inc(ffn_hi_made, 1)

            def make_xt_hi(b):
                for g, (h, d) in enumerate(XT_GROUPS):
                    act.wait_ge(xt_mm, NG * b + g + 1)
                    nc.scalar.activation(xt_hi[:, d, h * HALF:(h + 1) * HALF], xt_bank[g], ACT.Copy)\
                      .then_inc(xt_hi_made, 1)

            def make_yt_hi(b):
                for g, (h, d) in enumerate(XT_GROUPS):
                    act.wait_ge(yt_mm, NG * b + g + 1)
                    nc.scalar.activation(yt_hi[:, d, h * HALF:(h + 1) * HALF], g_ps[g % 2][:, :],
                                         ACT.Identity, bias=y_bias[:, d:d + 1]).then_inc(yt_hi_made, 1)

            def make_v_hi(b, n):
                act.wait_ge(vf_mm, TILES * b + n + 1)
                nc.scalar.activation(v_hl[:, n, 0:D], g_ps[n % 2][:, 0:D], ACT.Copy).then_inc(v_hi_made, 1)

            def make_p(b, t):
                act.wait_ge(exp_bias_made, TILES * b + t + 1)
                nc.scalar.activation(p[:, :], s_ps[:, :], ACT.Exp, bias=exp_bias[:, t:t + 1],
                                     accum_out=p_sum[:, t:t + 1]).then_inc(p_made, 1)

            def make_pt_hi(b, t):
                for h in range(2):
                    act.wait_ge(pt_mm, 2 * (TILES * b + t) + h + 1)
                    nc.scalar.activation(pt_hi[:, h * HT:(h + 1) * HT, :],
                                         t_ps[h][:, :].rearrange("p (n q) -> p n q", q=PT), ACT.Copy)\
                      .then_inc(pt_hi_made, 1)

            def batch(b, last):
                make_yt_hi(b)
                make_v_hi(b, 0)
                make_p(b, 0)
                for n in range(1, TILES):
                    make_v_hi(b, n)
                for t in range(TILES):
                    make_pt_hi(b, t)
                    if t + 1 < TILES:
                        make_p(b, t + 1)
                if not last:
                    make_xt_hi(b + 1)

            make_xt_hi(0)
            act.wait_ge(from_bias_made, 1)
            batch(0, last=False)
            with act.Fori(1, B - 1) as b:
                batch(b, last=False)
            batch(B - 1, last=True)

        @block.vector
        def _(dve):
            dve.wait_ge(qk_loaded, 4 * DMA)
            for o in range(DT):
                nc.vector.tensor_copy(bk_wide[:, o, :], bk_col[:, o:o + 1].to_broadcast([PT, PT]))\
                  .then_inc(bk_spread, 1)

            def make_stats(b, tiles):
                for n in tiles:
                    nc.vector.bn_stats(stats[:, n, :], x_sb[:, n, :]).then_inc(stats_made, 1)

            def make_mean_var(b):
                for n in range(TILES):
                    nc.vector.bn_aggr(mean_var[:, n, :], stats[:, n, :]).then_inc(mean_var_made, 1)

            def make_xn(b, tiles):
                dve.wait_ge(rstd_made, b + 1)
                wait(dve, xt_mm, NG * b)
                wait(dve, prod_made, 2 * b)
                for n in tiles:
                    nc.vector.tensor_scalar(xn[:, n, :], x_sb[:, n, :], mean_var[:, n, 0:1], rstd[:, n:n + 1],
                                            ALU.subtract, ALU.mult).then_inc(xn_made, 1)

            def make_xt_lo(b, groups):
                for g in groups:
                    h, d = XT_GROUPS[g]
                    dve.wait_ge(xt_hi_made, NG * b + g + 1)
                    t = slice(h * HALF, (h + 1) * HALF)
                    nc.vector.tensor_tensor(xt_lo[:, d, t], xt_bank[g], xt_hi[:, d, t].bitcast(f32),
                                            ALU.subtract).then_inc(xt_lo_made, 1)

            for j in range(4):
                dve.wait_ge(x0_loaded[j], DMA)
                make_stats(0, range(j * TILES // 4, (j + 1) * TILES // 4))
            dve.wait_ge(stats_made, TILES)
            make_mean_var(0)

            dve.wait_ge(a_hi_made, 1)
            nc.vector.scalar_tensor_tensor(a_lo[:, :, :].rearrange("p t n -> p (t n)"), s_ps[:, 0:512], SCALE,
                                           a_hi[:, :, :].rearrange("p t n -> p (t n)").bitcast(f32),
                                           ALU.mult, ALU.subtract).then_inc(a_lo_made, 1)
            dve.wait_ge(from_bias_mm, 1)
            nc.vector.tensor_scalar(from_bias[:, :], o_ps[0][:, 0:D + DT + 1], SCALE, None, ALU.mult)\
              .then_inc(from_bias_made, 1)
            dve.wait_ge(wv_hi_made, 1)
            nc.vector.tensor_tensor(vf_lo[:, :, 0:D], s_ps[:, 512:1024].rearrange("p (t n) -> p t n", t=DT),
                                    vf_hi[:, :, 0:D].bitcast(f32), ALU.subtract).then_inc(wv_lo_made, 1)
            make_xn(0, range(TILES))
            dve.wait_ge(full_mm, 1)
            dve.wait_ge(ffn_w_t_made, 1)
            nc.vector.tensor_tensor(ffn_full_t[:, :, :], o_ps[1][:, :].rearrange("p (t n) -> p t n", t=DT),
                                    ffn_w_t[:, :, :], ALU.add).then_inc(ffn_full_made, 1)
            dve.wait_ge(ffn_hi_made, 1)
            nc.vector.tensor_tensor(vf_lo[:, :, D:2 * D], ffn_full_t[:, :, :],
                                    vf_hi[:, :, D:2 * D].bitcast(f32), ALU.subtract).then_inc(ffn_lo_made, 1)
            make_xt_lo(0, range(NG))
            dve.wait_ge(from_bias_made, 1)

            def make_c(b, h):
                dve.wait_ge(prod_made, 2 * b + h + 1)
                nc.vector.tensor_reduce(c_sum[:, h * HT:(h + 1) * HT], prod[:, h * HT:(h + 1) * HT, :],
                                        AX.X, ALU.add).then_inc(c_sum_made, 1)

            def add_c_const(b):
                dve.wait_ge(c_sum_made, 2 * b + 2)
                nc.vector.tensor_scalar(c[:, :], c_sum[:, :], c_const, None, ALU.add).then_inc(c_made, 1)

            def make_yt_lo(b, g):
                h, d = XT_GROUPS[g]
                t = slice(h * HALF, (h + 1) * HALF)
                dve.wait_ge(yt_hi_made, NG * b + g + 1)
                nc.vector.scalar_tensor_tensor(yt_lo[:, d, t], g_ps[g % 2][:, :], y_bias[:, d:d + 1],
                                               yt_hi[:, d, t].bitcast(f32), ALU.add, ALU.subtract)\
                  .then_inc(yt_lo_made, 1)

            def make_v_lo_and_base(b, n):
                dve.wait_ge(v_hi_made, TILES * b + n + 1)
                nc.vector.tensor_tensor(v_hl[:, n, D:2 * D], g_ps[n % 2][:, 0:D],
                                        v_hl[:, n, 0:D].bitcast(f32), ALU.subtract).then_inc(v_lo_made, 1)
                if n == 0:
                    dve.wait_ge(x_bias_made, b + 1)
                nc.vector.tensor_tensor(base[:, n, :], g_ps[n % 2][:, D:2 * D], x_bias[:, n, :], ALU.add)\
                  .then_inc(base_made, 1)

            def make_exp_bias(b, t):
                for h in range(2):
                    dve.wait_ge(score_mm, 2 * (TILES * b + t) + h + 1)
                    nc.vector.tensor_reduce(half_max[:, t, h:h + 1], s_ps[:, h * 512:(h + 1) * 512],
                                            AX.X, ALU.max).then_inc(half_max_made, 1)
                dve.wait_ge(half_max_made, 2 * (TILES * b + t) + 2)
                if t == 0:
                    dve.wait_ge(c_made, b + 1)
                nc.vector.scalar_tensor_tensor(full_max[:, t:t + 1], half_max[:, t, 0:1], half_max[:, t, 1:2],
                                               c[:, t:t + 1], ALU.max, ALU.add).then_inc(full_max_made, 1)
                dve.wait_ge(full_max_made, TILES * b + t + 1)
                nc.vector.tensor_tensor(exp_bias[:, t:t + 1], c[:, t:t + 1], full_max[:, t:t + 1], ALU.subtract)\
                  .then_inc(exp_bias_made, 1)

            def make_pt_lo(b, t):
                for h in range(2):
                    dve.wait_ge(pt_hi_made, 2 * (TILES * b + t) + h + 1)
                    n = slice(h * HT, (h + 1) * HT)
                    nc.vector.tensor_tensor(pt_lo[:, n, :], t_ps[h][:, :].rearrange("p (n q) -> p n q", q=PT),
                                            pt_hi[:, n, :].bitcast(f32), ALU.subtract).then_inc(pt_lo_made, 1)
                dve.wait_ge(p_made, TILES * b + t + 1)
                nc.vector.reciprocal(p_sum_inv[:, t:t + 1], p_sum[:, t:t + 1]).then_inc(inv_made, 1)

            def make_out(b, t):
                dve.wait_ge(pv_mm, TILES * b + t + 1)
                dve.wait_ge(inv_made, TILES * b + t + 1)
                nc.vector.scalar_tensor_tensor(with_low[:, t % 2, :], o_ps[t % 2][:, D:2 * D],
                                               p_sum_inv[:, t:t + 1], base[:, t, :], ALU.mult, ALU.add)\
                  .then_inc(with_low_made, 1)
                dve.wait_ge(with_low_made, TILES * b + t + 1)
                wait(dve, stored[t // 2], DMA * b)
                nc.vector.scalar_tensor_tensor(out_sb[:, t, :], o_ps[t % 2][:, 0:D], p_sum_inv[:, t:t + 1],
                                               with_low[:, t % 2, :], ALU.mult, ALU.add).then_inc(out_made, 1)

            def next_layer_norm(b, t):
                if t == 0:
                    dve.wait_ge(x_loaded, DMA * b)
                if t < 3:
                    make_stats(b, [range(0, 3), range(3, 6), range(6, 8)][t])
                elif t == 3:
                    make_mean_var(b)
                elif t < 7:
                    make_xn(b, [range(0, 2), range(2, 5), range(5, 8)][t - 4])

            def batch(b, last):
                make_yt_lo(b, 0)
                make_yt_lo(b, 1)
                make_c(b, 0)
                make_yt_lo(b, 2)
                make_c(b, 1)
                make_yt_lo(b, 3)
                add_c_const(b)
                make_exp_bias(b, 0)
                for n in range(TILES):
                    make_v_lo_and_base(b, n)
                for t in range(TILES):
                    make_pt_lo(b, t)
                    if t + 1 < TILES:
                        make_exp_bias(b, t + 1)
                    elif not last:
                        make_xt_lo(b + 1, range(0, 2))
                    if t == 3 and not last:
                        dve.wait_ge(stats_made, TILES * (b + 2))
                    if t > 0:
                        make_out(b, t - 1)
                    if not last:
                        next_layer_norm(b + 1, t)
                if not last:
                    make_xt_lo(b + 1, range(2, NG))
                make_out(b, TILES - 1)

            batch(0, last=False)
            with dve.Fori(1, B - 1) as b:
                batch(b, last=False)
            batch(B - 1, last=True)

        @block.tensor
        def _(pe):
            pe.wait_ge(qk_loaded, 4 * DMA)
            for d in range(DT):
                for o in range(DT):
                    mm = nc.tensor.matmul(s_ps[:, d * D:(d + 1) * D], wq_sb[:, o, d * PT:(d + 1) * PT],
                                          wk_sb[:, o, :], start=(o == 0), stop=(o == DT - 1))
            mm.then_inc(a_mm, 1)
            pe.wait_ge(bk_spread, DT)
            for o in range(DT):
                nc.tensor.matmul(o_ps[0][:, 0:D], bk_wide[:, o, :], wq_sb[:, o, :],
                                 start=(o == 0), stop=(o == DT - 1))
            for d in range(DT):
                for o in range(DT):
                    nc.tensor.matmul(o_ps[0][:, D + d:D + d + 1], wk_sb[:, o, d * PT:(d + 1) * PT],
                                     bq_col[:, o:o + 1], start=(o == 0), stop=(o == DT - 1))
            for o in range(DT):
                mm = nc.tensor.matmul(o_ps[0][:, D + DT:D + DT + 1], bk_wide[:, o, :], bq_col[:, o:o + 1],
                                      start=(o == 0), stop=(o == DT - 1))
            mm.then_inc(from_bias_mm, 1)

            pe.wait_ge(lora_loaded, 4 * DMA)
            nc.tensor.matmul(o_ps[1][0:RANK, 0:D], lora_down_t[:, :], down_aux_sb[:, :],
                             start=True, stop=True).then_inc(low_rank_mm, 1)
            pe.wait_ge(identity_made, 1)
            for o in range(DT):
                mm = nc.tensor.transpose(t_ps[1][:, o * PT:(o + 1) * PT], up_aux_pad[:, o, :], identity[:, :])
            mm.then_inc(weights_mm, 1)
            pe.wait_ge(low_rank_made, 1)
            nc.tensor.matmul(o_ps[1][0:UDIM, D:2 * D], lora_up_t[:, :], low_rank[:, :],
                             start=True, stop=True).then_inc(mid_rank_mm, 1)
            pe.wait_ge(vw_loaded, 2 * DMA)
            for w_sb, w_ps in ((ffn_w_sb, t_ps[0][:, :]), (wv_sb, s_ps[:, 512:1024])):
                for d in range(DT):
                    for o in range(DT):
                        mm = nc.tensor.transpose(w_ps[:, d * D + o * PT:d * D + (o + 1) * PT],
                                                 w_sb[:, o, d * PT:(d + 1) * PT], identity[:, :])
                mm.then_inc(weights_mm, 1)
            pe.wait_ge(mid_rank_made, 1)
            pe.wait_ge(up_aux_t_made, 1)
            for d in range(DT):
                mm = nc.tensor.matmul(o_ps[1][:, d * D:(d + 1) * D], mid_rank[:, d * PT:(d + 1) * PT],
                                      up_aux_t[0:UDIM, :], start=True, stop=True)
            mm.then_inc(full_mm, 1)

            def transpose_x(b):
                wait(pe, base_made, TILES * b)
                for g, (h, d) in enumerate(XT_GROUPS):
                    if d == 0:
                        pe.wait_ge(xn_made, TILES * b + (h + 1) * HT)
                    for n in range(HT):
                        mm = nc.tensor.transpose(xt_bank[g][:, n * PT:(n + 1) * PT],
                                                 xn[:, h * HT + n, d * PT:(d + 1) * PT], identity[:, :])
                    mm.then_inc(xt_mm, 1)

            def split_products(ps, left_hi, left_lo, right_hi, right_lo):
                for d in range(DT):
                    nc.tensor.matmul(ps, left_hi(d), right_hi(d), start=(d == 0), stop=False)
                    nc.tensor.matmul(ps, left_hi(d), right_lo(d), start=False, stop=False)
                    mm = nc.tensor.matmul(ps, left_lo(d), right_hi(d), start=False, stop=(d == DT - 1))
                return mm

            def project_y(b):
                for g, (h, do) in enumerate(XT_GROUPS):
                    if do == 0:
                        pe.wait_ge(xt_lo_made, NG * b + 2 * h + 2)
                    if g >= 2:
                        pe.wait_ge(yt_lo_made, NG * b + g - 1)
                    t = slice(h * HALF, (h + 1) * HALF)
                    o = slice(do * PT, (do + 1) * PT)
                    split_products(g_ps[g % 2][:, :],
                                   lambda d: a_hi[:, d, o], lambda d: a_lo[:, d, o],
                                   lambda d: xt_hi[:, d, t], lambda d: xt_lo[:, d, t]).then_inc(yt_mm, 1)

            def project_vf(b, n):
                if n < 2:
                    pe.wait_ge(yt_lo_made, NG * b + n + 3)
                else:
                    pe.wait_ge(base_made, TILES * b + n - 1)
                t = slice(n * PT, (n + 1) * PT)
                split_products(g_ps[n % 2][:, :],
                               lambda d: xt_hi[:, d, t], lambda d: xt_lo[:, d, t],
                               lambda d: vf_hi[:, d, :], lambda d: vf_lo[:, d, :]).then_inc(vf_mm, 1)

            def scores(b, t):
                if t % HT == 0:
                    pe.wait_ge(yt_lo_made, NG * b + (2 if t == 0 else 4))
                if t == 0:
                    pe.wait_ge(xt_lo_made, NG * (b + 1))
                q = slice(t * PT, (t + 1) * PT)
                for h in range(2):
                    k = slice(h * HALF, (h + 1) * HALF)
                    split_products(s_ps[:, h * 512:(h + 1) * 512],
                                   lambda d: yt_hi[:, d, q], lambda d: yt_lo[:, d, q],
                                   lambda d: xt_hi[:, d, k], lambda d: xt_lo[:, d, k]).then_inc(score_mm, 1)

            def transpose_p(b, t):
                pe.wait_ge(p_made, TILES * b + t + 1)
                for h in range(2):
                    for n in range(HT):
                        mm = nc.tensor.transpose(t_ps[h][:, n * PT:(n + 1) * PT],
                                                 p[:, (h * HT + n) * PT:(h * HT + n + 1) * PT], identity[:, :])
                    mm.then_inc(pt_mm, 1)

            def p_times_v(b, t):
                if t == 0:
                    pe.wait_ge(v_lo_made, TILES * (b + 1))
                wait(pe, out_made, TILES * b + t - 1)
                for n in range(TILES):
                    if n % HT == 0:
                        pe.wait_ge(pt_lo_made, 2 * (TILES * b + t) + n // HT + 1)

                    def high():
                        return nc.tensor.matmul(o_ps[t % 2][:, :], pt_hi[:, n, :], v_hl[:, n, :],
                                                start=(n == 0), stop=(n == TILES - 1))
                    if n == 0:
                        high()
                    nc.tensor.matmul(o_ps[t % 2][:, 0:D], pt_lo[:, n, :], v_hl[:, n, 0:D],
                                     start=False, stop=False)
                    if n > 0:
                        mm = high()
                mm.then_inc(pv_mm, 1)

            def batch(b, last):
                project_y(b)
                scores(b, 0)
                for n in range(TILES):
                    project_vf(b, n)
                for t in range(TILES):
                    transpose_p(b, t)
                    if t + 1 < TILES:
                        scores(b, t + 1)
                    elif not last:
                        transpose_x(b + 1)
                    p_times_v(b, t)

            pe.wait_ge(a_lo_made, 1)
            pe.wait_ge(wv_lo_made, 1)
            transpose_x(0)
            pe.wait_ge(ffn_lo_made, 1)
            pe.wait_ge(from_bias_made, 1)
            batch(0, last=False)
            with pe.Fori(1, B - 1) as b:
                batch(b, last=False)
            batch(B - 1, last=True)


_INS = ["L0_attn_x", "L0_attn_wq", "L0_attn_bq", "L0_attn_wk", "L0_attn_bk", "L0_attn_wv", "L0_attn_bv",
        "L0_ffn_W", "L0_ffn_b", "L0_ffn_lora_down", "L0_ffn_lora_up", "L0_ffn_down_aux", "L0_ffn_up_aux"]


def kernel(**inputs):
    import numpy as _np
    import concourse.bacc as _bacc
    from concourse import mybir as _mybir
    from concourse.bass_utils import run_bass_kernel_spmd as _run

    nc = _bacc.Bacc("TRN2", target_bir_lowering=False, num_devices=1)
    arrays, args = {}, []
    for name in _INS:
        a = _np.ascontiguousarray(inputs[name])
        arrays[f"in_{name}"] = a
        args.append(nc.dram_tensor(f"in_{name}", a.shape, _mybir.dt.from_np(a.dtype), kind="ExternalInput").ap())
    shape = tuple(inputs["L0_attn_x"].shape)
    args.append(nc.dram_tensor("out_0", shape, _mybir.dt.float32, kind="ExternalOutput").ap())
    attention_plus_lora_ffn(nc, *args)
    r = _run(nc, [arrays], core_ids=[0])
    return r.results[0]["out_0"]
```

```python
import concourse.bass as bass
from concourse import mybir
from contextlib import ExitStack


def attention_plus_lora_ffn(
    nc: bass.Bass,
    x: bass.AP,
    wq: bass.AP,
    bq: bass.AP,
    wk: bass.AP,
    bk: bass.AP,
    wv: bass.AP,
    bv: bass.AP,
    ffn_w: bass.AP,
    ffn_b: bass.AP,
    lora_down: bass.AP,
    lora_up: bass.AP,
    down_aux: bass.AP,
    up_aux: bass.AP,
    out: bass.AP,
):
    f32 = mybir.dt.float32
    f32r = mybir.dt.float32r
    ALU = mybir.AluOpType
    ACT = mybir.ActivationFunctionType
    MAX = bass.bass_isa.ReduceOp.max

    B, S, D = x.shape
    PT = 128
    BANK = 512
    TILES = S // PT
    DT = D // PT
    CHUNKS = S // BANK
    CT = TILES // CHUNKS
    RING = 4
    ONES = 2
    BLOCKS = 8
    RANK, DDIM = lora_down.shape
    UDIM = lora_up.shape[0]
    SCALE = float(D) ** -0.5
    EPS = 1e-5
    DMA = 16

    x_v = x.rearrange("b (p n) d -> b p (n d)", n=TILES)
    out_v = out.rearrange("b (p n) d -> b p n d", n=TILES)

    def rows(w):
        return w.rearrange("(t p) n -> p t n", p=PT)

    def column(v):
        return v.rearrange("(t p) -> p t", p=PT)

    def row_for_all(v):
        return v.rearrange("(a n) -> a n", a=1).partition_broadcast(PT).rearrange("p a n -> p (a n)")

    ctx = ExitStack()
    with ctx:
        def sb(name, shape, dt=f32):
            return ctx.enter_context(nc.sbuf_tensor(name, shape, dt))

        def bank(name):
            return ctx.enter_context(nc.psum_tensor(name, [PT, BANK], f32))

        def sem(name):
            return ctx.enter_context(nc.semaphore(name))

        bq_col = sb("bq_col", [PT, DT])
        bk_col = sb("bk_col", [PT, DT])
        bias_all = sb("bias_all", [PT, D])
        lora_down_t = sb("lora_down_t", [DDIM, RANK])
        lora_up_t = sb("lora_up_t", [RANK, UDIM])
        identity = sb("identity", [PT, PT])
        minus_half = sb("minus_half", [PT, TILES])
        eps_all = sb("eps_all", [PT, TILES])
        a_hi = sb("a_hi", [PT, DT, D], f32r)
        a_lo = sb("a_lo", [PT, DT, D], f32r)
        vf_hi = sb("vf_hi", [PT, DT, 2 * D], f32r)
        vf_lo = sb("vf_lo", [PT, DT, 2 * D], f32r)
        from_bias = sb("from_bias", [PT, D + DT + 1])
        e_row = from_bias[:, 0:D]
        z_bias = from_bias[:, D:D + DT]
        e_const = from_bias[:, D + DT:D + DT + 1]

        x_sb = sb("x_sb", [PT, TILES, D])
        xn = sb("xn", [PT, TILES, D])
        x_bias = sb("x_bias", [PT, TILES, D])
        prod = sb("prod", [PT, TILES, D])
        base = sb("base", [PT, TILES, D])
        stats = sb("stats", [PT, TILES, 6])
        mean_var = sb("mean_var", [PT, TILES, 2])
        var_eps = sb("var_eps", [PT, TILES])
        rstd = sb("rstd", [PT, TILES])
        e_sum = sb("e_sum", [PT, TILES])
        e = sb("e", [PT, TILES])
        xt_hi = sb("xt_hi", [PT, DT, S], f32r)
        xt_lo = sb("xt_lo", [PT, DT, S], f32r)
        zt_hi = sb("zt_hi", [PT, DT, S], f32r)
        zt_lo = sb("zt_lo", [PT, DT, S], f32r)
        v_hi = sb("v_hi", [PT, TILES, D + ONES], f32r)
        v_lo = sb("v_lo", [PT, TILES, D], f32r)
        p_sum_inv = sb("p_sum_inv", [PT, TILES])
        s = [sb(f"s{c}", [PT, TILES, BANK]) for c in range(CHUNKS)]
        p_hi = [sb(f"p_hi{c}", [PT, TILES, BANK], f32r) for c in range(CHUNKS)]
        p_lo = [sb(f"p_lo{c}", [PT, TILES, BANK], f32r) for c in range(CHUNKS)]
        down_aux_sb = s[0][0:DDIM, 0, 0:D]
        up_aux_pad = s[0][:, 0, D:2 * D].rearrange("p (t n) -> p t n", t=DT)
        low_rank = s[0][0:RANK, 1, 0:D]
        mid_rank = s[0][0:UDIM, 1, D:2 * D]
        early = s[CHUNKS - 1]
        wk_sb, wq_sb, wv_sb, ffn_w_sb, ffn_w_t, ffn_full_t = (
            early[:, i, :].rearrange("p (t n) -> p t n", t=DT) for i in range(6))
        bv_all, ffn_b_all = (early[:, 6, i * D:(i + 1) * D] for i in range(2))
        up_aux_t = early[:, 7, 0:D]
        bq_wide = early[:, 7, D:2 * D].rearrange("p (t n) -> p t n", t=DT)
        tile_max = [sb(f"tile_max{c}", [PT, BANK]) for c in range(CHUNKS)]
        top = [sb(f"top{c}", [PT, BANK]) for c in range(CHUNKS)]

        gate = sb("gate", [PT, 1])

        s_ps = [bank(f"s_ps{i}") for i in range(RING)]
        o_ps = [bank(f"o_ps{i}") for i in range(2)]
        g_ps = [bank(f"g_ps{i}") for i in range(2)]

        x0_loaded = [sem(f"x0_loaded{j}") for j in range(4)]
        x_loaded = sem("x_loaded")
        qk_loaded = sem("qk_loaded")
        lora_loaded = sem("lora_loaded")
        vw_loaded = sem("vw_loaded")
        bias_loaded = sem("bias_loaded")
        stored = [sem(f"stored{j}") for j in range(TILES // 2)]
        zeroed = sem("zeroed")
        ones_made = sem("ones_made")
        identity_made = sem("identity_made")
        bq_spread = sem("bq_spread")
        bias_made = sem("bias_made")
        a_mm = sem("a_mm")
        from_bias_mm = sem("from_bias_mm")
        weights_mm = sem("weights_mm")
        low_rank_mm = sem("low_rank_mm")
        mid_rank_mm = sem("mid_rank_mm")
        full_mm = sem("full_mm")
        a_hi_made = sem("a_hi_made")
        a_lo_made = sem("a_lo_made")
        from_bias_made = sem("from_bias_made")
        wv_hi_made = sem("wv_hi_made")
        wv_lo_made = sem("wv_lo_made")
        low_rank_made = sem("low_rank_made")
        up_aux_t_made = sem("up_aux_t_made")
        mid_rank_made = sem("mid_rank_made")
        ffn_w_t_made = sem("ffn_w_t_made")
        ffn_full_made = sem("ffn_full_made")
        ffn_hi_made = sem("ffn_hi_made")
        ffn_lo_made = sem("ffn_lo_made")
        stats_made = sem("stats_made")
        mean_var_made = sem("mean_var_made")
        var_eps_made = sem("var_eps_made")
        rstd_made = sem("rstd_made")
        xn_made = sem("xn_made")
        x_bias_made = sem("x_bias_made")
        prod_made = sem("prod_made")
        e_sum_made = sem("e_sum_made")
        e_made = sem("e_made")
        xt_mm = sem("xt_mm")
        xt_hi_made = sem("xt_hi_made")
        xt_lo_made = sem("xt_lo_made")
        zt_mm = sem("zt_mm")
        zt_hi_made = sem("zt_hi_made")
        zt_lo_made = sem("zt_lo_made")
        vf_mm = sem("vf_mm")
        v_hi_made = sem("v_hi_made")
        v_lo_made = sem("v_lo_made")
        base_made = sem("base_made")
        score_mm = sem("score_mm")
        tile_max_made = sem("tile_max_made")
        s_made = sem("s_made")
        gate_made = sem("gate_made")
        top_made = sem("top_made")
        shifted = sem("shifted")
        p_made = sem("p_made")
        p_hi_made = sem("p_hi_made")
        p_lo_made = sem("p_lo_made")
        pv_mm = sem("pv_mm")
        inv_made = sem("inv_made")
        out_made = sem("out_made")

        def wait(eng, semaphore, count):
            if isinstance(count, int) and count <= 0:
                return
            eng.wait_ge(semaphore, count)

        GROUPS = [(h, d) for h in range(2) for d in range(DT)]
        NG = len(GROUPS)
        xt_bank = [g_ps[0], g_ps[1], s_ps[0], s_ps[1]]
        zt_bank = [g_ps[0], g_ps[1], s_ps[2], s_ps[3]]
        vf_bank = [g_ps[0], g_ps[1], o_ps[0], o_ps[1]]
        NV = len(vf_bank)
        HT = TILES // 2

        def half(h):
            return slice(h * (S // 2), (h + 1) * (S // 2))

        def two(ap):
            return ap.rearrange("p (t n) -> p t n", t=DT)

        HQ = BANK // 2
        PAIRS = TILES // 2

        def block_of(j):
            h, pair = divmod(j, PAIRS)
            return slice(2 * pair, 2 * pair + 2), slice(h * HQ, (h + 1) * HQ)

        block = ctx.enter_context(nc.Block())

        @block.sync
        def _(sp):
            for j in range(4):
                n = TILES // 4
                sp.dma_start(x_sb[:, j * n:(j + 1) * n, :],
                             x_v[0, :, j * n * D:(j + 1) * n * D].rearrange("p (n d) -> p n d", d=D))\
                  .then_inc(x0_loaded[j], DMA)

            def load(b):
                sp.wait_ge(xn_made, TILES * b)
                sp.wait_ge(x_bias_made, b)
                sp.dma_start(x_sb[:, :, :], x_v[b, :, :].rearrange("p (n d) -> p n d", d=D))\
                  .then_inc(x_loaded, DMA)

            def store(b, j):
                sp.wait_ge(out_made, TILES * b + 2 * j + 2)
                sp.dma_start(out_v[b, :, 2 * j:2 * j + 2, :], base[:, 2 * j:2 * j + 2, :])\
                  .then_inc(stored[j], DMA)

            load(1)
            with sp.Fori(0, B - 2) as b:
                for j in range(CT // 2):
                    store(b, j)
                load(b + 2)
                for j in range(CT // 2, TILES // 2):
                    store(b, j)
            for b in range(B - 2, B):
                for j in range(TILES // 2):
                    store(b, j)
            for j in range(TILES // 2):
                sp.wait_ge(stored[j], DMA * B)

        @block.gpsimd
        def _(pool):
            nc.gpsimd.memset(identity[:, :], 0.0).then_inc(zeroed, 1)
            nc.gpsimd.memset(up_aux_pad[:, :, :], 0.0).then_inc(zeroed, 1)
            nc.gpsimd.memset(minus_half[:, :], -0.5).then_inc(zeroed, 1)
            nc.gpsimd.memset(eps_all[:, :], EPS).then_inc(zeroed, 1)
            pool.wait_ge(zeroed, 1)
            nc.gpsimd.affine_select(out=identity[:, :], in_=identity[:, :], compare_op=ALU.not_equal, fill=1.0,
                                    base=0, pattern=[[-1, PT]], channel_multiplier=1).then_inc(identity_made, 1)
            nc.gpsimd.memset(v_hi[:, :, D:D + ONES].bitcast(f32), 1.0).then_inc(ones_made, 1)
            pool.wait_ge(bias_loaded, 2 * DMA)
            nc.gpsimd.tensor_tensor(bias_all[:, :], bv_all[:, :], ffn_b_all[:, :], ALU.add).then_inc(bias_made, 1)
            pool.wait_ge(bias_made, 1)
            pool.wait_ge(zeroed, 4)

            def make_rstd(b):
                pool.wait_ge(mean_var_made, TILES * (b + 1))
                nc.gpsimd.tensor_tensor(var_eps[:, :], mean_var[:, :, 1], eps_all[:, :], ALU.add)\
                  .then_inc(var_eps_made, 1)
                pool.wait_ge(var_eps_made, b + 1)
                nc.gpsimd.tensor_tensor(rstd[:, :], var_eps[:, :], minus_half[:, :], ALU.pow)\
                  .then_inc(rstd_made, 1)

            def make_x_bias(b):
                wait(pool, base_made, TILES * b)
                nc.gpsimd.tensor_tensor(x_bias[:, :, :], x_sb[:, :, :],
                                        bias_all[:, :].unsqueeze(1).to_broadcast([PT, TILES, D]), ALU.add)\
                  .then_inc(x_bias_made, 1)

            def make_prod(b):
                wait(pool, e_sum_made, TILES * b)
                for i in range(TILES // 2):
                    pool.wait_ge(xn_made, TILES * b + 2 * i + 2)
                    nc.gpsimd.tensor_tensor(prod[:, 2 * i:2 * i + 2, :], xn[:, 2 * i:2 * i + 2, :],
                                            e_row.unsqueeze(1).to_broadcast([PT, 2, D]), ALU.mult)\
                      .then_inc(prod_made, 1)

            def make_top(b, c):
                wait(pool, gate_made, CHUNKS * b + c)
                pool.wait_ge(tile_max_made, TILES * (CHUNKS * b + c + 1))
                nc.gpsimd.tensor_tensor(gate[:, :], tile_max[c][:, 0:1], tile_max[c][:, 0:1], ALU.add)\
                  .then_inc(gate_made, 1)
                for h in range(2):
                    q = slice(h * HQ, (h + 1) * HQ)
                    nc.gpsimd.partition_all_reduce(top[c][:, q], tile_max[c][:, q], PT, MAX).then_inc(top_made, 1)

            def batch(b, last):
                if not last:
                    pool.wait_ge(x_loaded, DMA * (b + 1))
                    make_rstd(b + 1)
                make_top(b, 0)
                if not last:
                    make_prod(b + 1)
                make_top(b, 1)
                if not last:
                    make_x_bias(b + 1)

            for j in range(4):
                pool.wait_ge(x0_loaded[j], DMA)
            make_rstd(0)
            make_x_bias(0)
            pool.wait_ge(from_bias_made, 1)
            make_prod(0)
            batch(0, last=False)
            with pool.Fori(1, B - 1) as b:
                batch(b, last=False)
            batch(B - 1, last=True)

        @block.scalar
        def _(act):
            act.dma_start(wk_sb[:, :, :], rows(wk)).then_inc(qk_loaded, DMA)
            act.dma_start(wq_sb[:, :, :], rows(wq)).then_inc(qk_loaded, DMA)
            with nc.allow_non_contiguous_dma(reason="a few hundred words of biases and LoRA factors"):
                act.dma_start(bq_col[:, :], column(bq)).then_inc(qk_loaded, DMA)
                act.dma_start(bk_col[:, :], column(bk)).then_inc(qk_loaded, DMA)
                act.dma_start(lora_down_t[:, :], lora_down.rearrange("r d -> d r")).then_inc(lora_loaded, DMA)
                act.dma_start(lora_up_t[:, :], lora_up.rearrange("u r -> r u")).then_inc(lora_loaded, DMA)
            act.dma_start(down_aux_sb[:, :], down_aux).then_inc(lora_loaded, DMA)
            act.wait_ge(zeroed, 2)
            act.dma_start(up_aux_pad[:, :, 0:UDIM], rows(up_aux)).then_inc(lora_loaded, DMA)
            act.dma_start(wv_sb[:, :, :], rows(wv)).then_inc(vw_loaded, DMA)
            act.dma_start(ffn_w_sb[:, :, :], rows(ffn_w)).then_inc(vw_loaded, DMA)
            act.dma_start(bv_all[:, :], row_for_all(bv)).then_inc(bias_loaded, DMA)
            act.dma_start(ffn_b_all[:, :], row_for_all(ffn_b)).then_inc(bias_loaded, DMA)

            act.wait_ge(a_mm, 1)
            nc.scalar.activation(a_hi[:, :, :], two(s_ps[0][:, :]), ACT.Copy, scale=SCALE).then_inc(a_hi_made, 1)
            act.wait_ge(low_rank_mm, 1)
            nc.scalar.activation(low_rank[:, :], o_ps[1][0:RANK, 0:D], ACT.Copy).then_inc(low_rank_made, 1)
            act.wait_ge(mid_rank_mm, 1)
            nc.scalar.activation(mid_rank[:, :], o_ps[1][0:UDIM, D:2 * D], ACT.Copy).then_inc(mid_rank_made, 1)
            act.wait_ge(weights_mm, 1)
            nc.scalar.activation(up_aux_t[:, :], s_ps[3][:, 0:D], ACT.Copy).then_inc(up_aux_t_made, 1)
            act.wait_ge(weights_mm, 2)
            nc.scalar.activation(ffn_w_t[:, :, :], two(s_ps[2][:, :]), ACT.Copy).then_inc(ffn_w_t_made, 1)
            act.wait_ge(weights_mm, 3)
            nc.scalar.activation(vf_hi[:, :, 0:D], two(s_ps[1][:, :]), ACT.Copy).then_inc(wv_hi_made, 1)
            act.wait_ge(ffn_full_made, 1)
            nc.scalar.activation(vf_hi[:, :, D:2 * D], ffn_full_t[:, :, :], ACT.Copy).then_inc(ffn_hi_made, 1)

            def make_xt_hi(b):
                for g, (h, d) in enumerate(GROUPS):
                    act.wait_ge(xt_mm, NG * b + g + 1)
                    nc.scalar.activation(xt_hi[:, d, half(h)], xt_bank[g][:, :], ACT.Copy).then_inc(xt_hi_made, 1)

            def make_e(b):
                for n in range(TILES):
                    if n % 2 == 0:
                        act.wait_ge(prod_made, TILES // 2 * b + n // 2 + 1)
                    nc.scalar.activation(prod[:, n, :], prod[:, n, :], ACT.Copy,
                                         accum_out=e_sum[:, n:n + 1]).then_inc(e_sum_made, 1)
                act.wait_ge(e_sum_made, TILES * (b + 1))
                nc.scalar.activation(e[:, :], e_sum[:, :], ACT.Identity, bias=e_const).then_inc(e_made, 1)

            def make_zt_hi(b):
                for g, (h, d) in enumerate(GROUPS):
                    act.wait_ge(zt_mm, NG * b + g + 1)
                    nc.scalar.activation(zt_hi[:, d, half(h)], zt_bank[g][:, :], ACT.Identity,
                                         bias=z_bias[:, d:d + 1]).then_inc(zt_hi_made, 1)

            def make_v_hi(b, n):
                act.wait_ge(vf_mm, TILES * b + n + 1)
                nc.scalar.activation(v_hi[:, n, 0:D], vf_bank[n % NV][:, 0:D], ACT.Copy).then_inc(v_hi_made, 1)

            def make_s(b, c, n):
                act.wait_ge(tile_max_made, TILES * (CHUNKS * b + c) + n + 1)
                nc.scalar.activation(s[c][:, n, :], s_ps[n % RING][:, :], ACT.Identity, bias=e[:, n:n + 1])\
                  .then_inc(s_made, 1)

            def make_p(b, c, j):
                keys, q = block_of(j)
                act.wait_ge(shifted, BLOCKS * (CHUNKS * b + c) + j + 1)
                nc.scalar.activation(s[c][:, keys, q], s[c][:, keys, q], ACT.Exp).then_inc(p_made, 1)

            def make_p_hi(b, c, j):
                keys, q = block_of(j)
                act.wait_ge(p_made, BLOCKS * (CHUNKS * b + c) + j + 1)
                nc.scalar.activation(p_hi[c][:, keys, q], s[c][:, keys, q], ACT.Copy).then_inc(p_hi_made, 1)

            def batch(b, last):
                make_zt_hi(b)
                for n in range(TILES):
                    make_s(b, 0, n)
                for n in range(TILES):
                    make_v_hi(b, n)
                    if n >= 4:
                        make_p(b, 0, n - 4)
                    if n >= 5:
                        make_p_hi(b, 0, n - 5)
                make_p_hi(b, 0, 3)
                for n in range(TILES):
                    make_s(b, 1, n)
                    if n >= 4:
                        make_p(b, 0, n)
                    if n >= 5:
                        make_p_hi(b, 0, n - 1)
                make_p_hi(b, 0, 7)
                for j in range(BLOCKS):
                    make_p(b, 1, j)
                    if j % PAIRS > 0:
                        make_p_hi(b, 1, j - 1)
                    if j % PAIRS == PAIRS - 1:
                        make_p_hi(b, 1, j)
                if not last:
                    make_xt_hi(b + 1)
                    make_e(b + 1)

            make_xt_hi(0)
            act.wait_ge(from_bias_made, 1)
            make_e(0)
            batch(0, last=False)
            with act.Fori(1, B - 1) as b:
                batch(b, last=False)
            batch(B - 1, last=True)

        @block.vector
        def _(dve):
            dve.wait_ge(qk_loaded, 4 * DMA)
            for o in range(DT):
                nc.vector.tensor_copy(bq_wide[:, o, :], bq_col[:, o:o + 1].to_broadcast([PT, PT]))\
                  .then_inc(bq_spread, 1)

            def make_stats(b, tiles):
                for n in tiles:
                    nc.vector.bn_stats(stats[:, n, :], x_sb[:, n, :]).then_inc(stats_made, 1)

            def make_mean_var(b):
                for n in range(TILES):
                    nc.vector.bn_aggr(mean_var[:, n, :], stats[:, n, :]).then_inc(mean_var_made, 1)

            def make_xn(b, tiles):
                dve.wait_ge(rstd_made, b + 1)
                wait(dve, xt_mm, NG * b)
                wait(dve, prod_made, TILES // 2 * b)
                for n in tiles:
                    nc.vector.tensor_scalar(xn[:, n, :], x_sb[:, n, :], mean_var[:, n, 0:1], rstd[:, n:n + 1],
                                            ALU.subtract, ALU.mult).then_inc(xn_made, 1)

            def make_xt_lo(b):
                for g, (h, d) in enumerate(GROUPS):
                    dve.wait_ge(xt_hi_made, NG * b + g + 1)
                    nc.vector.tensor_tensor(xt_lo[:, d, half(h)], xt_bank[g][:, :],
                                            xt_hi[:, d, half(h)].bitcast(f32), ALU.subtract).then_inc(xt_lo_made, 1)

            for j in range(4):
                dve.wait_ge(x0_loaded[j], DMA)
                make_stats(0, range(j * TILES // 4, (j + 1) * TILES // 4))
            dve.wait_ge(stats_made, TILES)
            make_mean_var(0)

            dve.wait_ge(a_hi_made, 1)
            nc.vector.scalar_tensor_tensor(a_lo[:, :, :].rearrange("p t n -> p (t n)"), s_ps[0][:, :], SCALE,
                                           a_hi[:, :, :].rearrange("p t n -> p (t n)").bitcast(f32),
                                           ALU.mult, ALU.subtract).then_inc(a_lo_made, 1)
            dve.wait_ge(from_bias_mm, 1)
            nc.vector.tensor_scalar(from_bias[:, :], o_ps[0][:, 0:D + DT + 1], SCALE, None, ALU.mult)\
              .then_inc(from_bias_made, 1)
            make_xn(0, range(TILES))
            dve.wait_ge(wv_hi_made, 1)
            nc.vector.tensor_tensor(vf_lo[:, :, 0:D], two(s_ps[1][:, :]), vf_hi[:, :, 0:D].bitcast(f32),
                                    ALU.subtract).then_inc(wv_lo_made, 1)
            dve.wait_ge(full_mm, 1)
            dve.wait_ge(ffn_w_t_made, 1)
            nc.vector.tensor_tensor(ffn_full_t[:, :, :], two(o_ps[1][:, :]), ffn_w_t[:, :, :], ALU.add)\
              .then_inc(ffn_full_made, 1)
            dve.wait_ge(ffn_hi_made, 1)
            nc.vector.tensor_tensor(vf_lo[:, :, D:2 * D], ffn_full_t[:, :, :],
                                    vf_hi[:, :, D:2 * D].bitcast(f32), ALU.subtract).then_inc(ffn_lo_made, 1)
            make_xt_lo(0)
            dve.wait_ge(from_bias_made, 1)

            def make_zt_lo(b):
                for g, (h, d) in enumerate(GROUPS):
                    dve.wait_ge(zt_hi_made, NG * b + g + 1)
                    nc.vector.scalar_tensor_tensor(zt_lo[:, d, half(h)], zt_bank[g][:, :], z_bias[:, d:d + 1],
                                                   zt_hi[:, d, half(h)].bitcast(f32), ALU.add, ALU.subtract)\
                      .then_inc(zt_lo_made, 1)

            def make_v_lo_and_base(b, n):
                dve.wait_ge(v_hi_made, TILES * b + n + 1)
                nc.vector.tensor_tensor(v_lo[:, n, :], vf_bank[n % NV][:, 0:D], v_hi[:, n, 0:D].bitcast(f32),
                                        ALU.subtract).then_inc(v_lo_made, 1)
                if n == 0:
                    dve.wait_ge(x_bias_made, b + 1)
                wait(dve, stored[n // 2], DMA * b)
                nc.vector.tensor_tensor(base[:, n, :], vf_bank[n % NV][:, D:2 * D], x_bias[:, n, :], ALU.add)\
                  .then_inc(base_made, 1)

            def make_tile_max(b, c, n):
                i = TILES * (CHUNKS * b + c) + n
                if n == 0:
                    dve.wait_ge(e_made, b + 1)
                    dve.wait_ge(score_mm, i + 1)
                    nc.vector.tensor_scalar(tile_max[c][:, :], s_ps[0][:, :], e[:, 0:1], None, ALU.add)\
                      .then_inc(tile_max_made, 1)
                else:
                    dve.wait_ge(tile_max_made, i)
                    dve.wait_ge(score_mm, i + 1)
                    nc.vector.scalar_tensor_tensor(tile_max[c][:, :], s_ps[n % RING][:, :], e[:, n:n + 1],
                                                   tile_max[c][:, :], ALU.add, ALU.max).then_inc(tile_max_made, 1)

            def shift(b, c, j):
                keys, q = block_of(j)
                dve.wait_ge(s_made, TILES * (CHUNKS * b + c) + keys.stop)
                if j % PAIRS == 0:
                    dve.wait_ge(top_made, 2 * (CHUNKS * b + c) + j // PAIRS + 1)
                nc.vector.tensor_tensor(s[c][:, keys, q], s[c][:, keys, q],
                                        top[c][:, q].unsqueeze(1).to_broadcast([PT, 2, HQ]), ALU.subtract)\
                  .then_inc(shifted, 1)

            def make_p_lo(b, c, j):
                keys, q = block_of(j)
                dve.wait_ge(p_hi_made, BLOCKS * (CHUNKS * b + c) + j + 1)
                nc.vector.tensor_tensor(p_lo[c][:, keys, q], s[c][:, keys, q], p_hi[c][:, keys, q].bitcast(f32),
                                        ALU.subtract).then_inc(p_lo_made, 1)

            def make_out(b, t):
                dve.wait_ge(pv_mm, TILES * b + t + 1)
                nc.vector.reciprocal(p_sum_inv[:, t:t + 1], o_ps[t % 2][:, D:D + 1]).then_inc(inv_made, 1)
                dve.wait_ge(inv_made, TILES * b + t + 1)
                nc.vector.scalar_tensor_tensor(base[:, t, :], o_ps[t % 2][:, 0:D], p_sum_inv[:, t:t + 1],
                                               base[:, t, :], ALU.mult, ALU.add).then_inc(out_made, 1)

            def batch(b, last):
                make_zt_lo(b)
                for n in range(TILES):
                    if n == 4 and not last:
                        dve.wait_ge(stats_made, TILES * (b + 2))
                    make_tile_max(b, 0, n)
                    if last:
                        continue
                    if n == 0:
                        dve.wait_ge(x_loaded, DMA * (b + 1))
                    if n < 4:
                        make_stats(b + 1, range(2 * n, 2 * n + 2))
                    elif n == 4:
                        make_mean_var(b + 1)
                    elif n == 6:
                        make_xn(b + 1, range(0, 2))
                for n in range(TILES):
                    make_v_lo_and_base(b, n)
                    if n < 3 and not last:
                        make_xn(b + 1, range(2 * n + 2, 2 * n + 4))
                    if 3 <= n < 7:
                        shift(b, 0, n - 3)
                make_p_lo(b, 0, 0)
                for n in range(TILES):
                    make_tile_max(b, 1, n)
                    if n < 3:
                        make_p_lo(b, 0, n + 1)
                    elif n < 7:
                        shift(b, 0, n + 1)
                make_p_lo(b, 0, 4)
                make_p_lo(b, 0, 5)
                make_out(b, 0)
                make_p_lo(b, 0, 6)
                shift(b, 1, 0)
                make_p_lo(b, 0, 7)
                shift(b, 1, 1)
                make_out(b, 1)
                shift(b, 1, 2)
                shift(b, 1, 3)
                for i in range(PAIRS):
                    make_p_lo(b, 1, i)
                    shift(b, 1, PAIRS + i)
                    if i == 2:
                        make_out(b, 2)
                make_out(b, 3)
                make_p_lo(b, 1, PAIRS)
                make_p_lo(b, 1, PAIRS + 1)
                make_out(b, CT)
                make_p_lo(b, 1, PAIRS + 2)
                make_p_lo(b, 1, PAIRS + 3)
                if not last:
                    make_xt_lo(b + 1)
                for t in range(CT + 1, TILES):
                    make_out(b, t)

            batch(0, last=False)
            with dve.Fori(1, B - 1) as b:
                batch(b, last=False)
            batch(B - 1, last=True)

        @block.tensor
        def _(pe):
            pe.wait_ge(qk_loaded, 4 * DMA)
            for d in range(DT):
                for o in range(DT):
                    mm = nc.tensor.matmul(s_ps[0][:, d * D:(d + 1) * D], wk_sb[:, o, d * PT:(d + 1) * PT],
                                          wq_sb[:, o, :], start=(o == 0), stop=(o == DT - 1))
            mm.then_inc(a_mm, 1)
            pe.wait_ge(bq_spread, DT)
            for o in range(DT):
                nc.tensor.matmul(o_ps[0][:, 0:D], bq_wide[:, o, :], wk_sb[:, o, :],
                                 start=(o == 0), stop=(o == DT - 1))
            for d in range(DT):
                for o in range(DT):
                    nc.tensor.matmul(o_ps[0][:, D + d:D + d + 1], wq_sb[:, o, d * PT:(d + 1) * PT],
                                     bk_col[:, o:o + 1], start=(o == 0), stop=(o == DT - 1))
            for o in range(DT):
                mm = nc.tensor.matmul(o_ps[0][:, D + DT:D + DT + 1], bq_wide[:, o, :], bk_col[:, o:o + 1],
                                      start=(o == 0), stop=(o == DT - 1))
            mm.then_inc(from_bias_mm, 1)

            pe.wait_ge(lora_loaded, 4 * DMA)
            nc.tensor.matmul(o_ps[1][0:RANK, 0:D], lora_down_t[:, :], down_aux_sb[:, :],
                             start=True, stop=True).then_inc(low_rank_mm, 1)
            pe.wait_ge(identity_made, 1)
            for o in range(DT):
                mm = nc.tensor.transpose(s_ps[3][:, o * PT:(o + 1) * PT], up_aux_pad[:, o, :], identity[:, :])
            mm.then_inc(weights_mm, 1)
            pe.wait_ge(low_rank_made, 1)
            nc.tensor.matmul(o_ps[1][0:UDIM, D:2 * D], lora_up_t[:, :], low_rank[:, :],
                             start=True, stop=True).then_inc(mid_rank_mm, 1)
            pe.wait_ge(vw_loaded, 2 * DMA)
            for w_sb, w_ps in ((ffn_w_sb, s_ps[2]), (wv_sb, s_ps[1])):
                for d in range(DT):
                    for o in range(DT):
                        mm = nc.tensor.transpose(w_ps[:, d * D + o * PT:d * D + (o + 1) * PT],
                                                 w_sb[:, o, d * PT:(d + 1) * PT], identity[:, :])
                mm.then_inc(weights_mm, 1)
            pe.wait_ge(mid_rank_made, 1)
            pe.wait_ge(up_aux_t_made, 1)
            for d in range(DT):
                mm = nc.tensor.matmul(o_ps[1][:, d * D:(d + 1) * D], mid_rank[:, d * PT:(d + 1) * PT],
                                      up_aux_t[0:UDIM, :], start=True, stop=True)
            mm.then_inc(full_mm, 1)

            def transpose_x(b):
                wait(pe, base_made, TILES * b)
                wait(pe, s_made, CHUNKS * TILES * b)
                for g, (h, d) in enumerate(GROUPS):
                    if d == 0:
                        pe.wait_ge(xn_made, TILES * b + (h + 1) * HT)
                    for n in range(HT):
                        mm = nc.tensor.transpose(xt_bank[g][:, n * PT:(n + 1) * PT],
                                                 xn[:, h * HT + n, d * PT:(d + 1) * PT], identity[:, :])
                    mm.then_inc(xt_mm, 1)

            def split_products(ps, left_hi, left_lo, right_hi, right_lo):
                for d in range(DT):
                    nc.tensor.matmul(ps, left_hi(d), right_hi(d), start=(d == 0), stop=False)
                    nc.tensor.matmul(ps, left_hi(d), right_lo(d), start=False, stop=False)
                    mm = nc.tensor.matmul(ps, left_lo(d), right_hi(d), start=False, stop=(d == DT - 1))
                return mm

            def project_z(b):
                for g, (h, do) in enumerate(GROUPS):
                    if do == 0:
                        pe.wait_ge(xt_lo_made, NG * b + 2 * h + 2)
                    o = slice(do * PT, (do + 1) * PT)
                    split_products(zt_bank[g][:, :],
                                   lambda d: a_hi[:, d, o], lambda d: a_lo[:, d, o],
                                   lambda d: xt_hi[:, d, half(h)], lambda d: xt_lo[:, d, half(h)])\
                        .then_inc(zt_mm, 1)

            def project_vf(b, n):
                if n == 2:
                    wait(pe, out_made, TILES * b)
                if n >= NV:
                    pe.wait_ge(base_made, TILES * b + n - NV + 1)
                t = slice(n * PT, (n + 1) * PT)
                split_products(vf_bank[n % NV][:, :],
                               lambda d: xt_hi[:, d, t], lambda d: xt_lo[:, d, t],
                               lambda d: vf_hi[:, d, :], lambda d: vf_lo[:, d, :]).then_inc(vf_mm, 1)

            def scores(b, c):
                q = slice(c * BANK, (c + 1) * BANK)
                for n in range(TILES):
                    wait(pe, s_made, TILES * (CHUNKS * b + c) + n - RING + 1)
                    if c == 0 and n in (0, 2, 3):
                        pe.wait_ge(zt_lo_made, NG * b + max(n, 1) + 1)
                    k = slice(n * PT, (n + 1) * PT)
                    split_products(s_ps[n % RING][:, :],
                                   lambda d: zt_hi[:, d, k], lambda d: zt_lo[:, d, k],
                                   lambda d: xt_hi[:, d, q], lambda d: xt_lo[:, d, q]).then_inc(score_mm, 1)

            def p_times_v(b, t):
                c, q = t // CT, slice(t % CT * PT, (t % CT + 1) * PT)
                if t == 0:
                    pe.wait_ge(v_lo_made, TILES * (b + 1))
                    pe.wait_ge(base_made, TILES * (b + 1))
                elif t >= 2:
                    pe.wait_ge(out_made, TILES * b + t - 1)
                for n in range(TILES):
                    if t % 2 == 0 and n % 2 == 0:
                        pe.wait_ge(p_lo_made, BLOCKS * (CHUNKS * b + c) + t % CT // 2 * PAIRS + n // 2 + 1)
                    nc.tensor.matmul(o_ps[t % 2][:, 0:D + ONES], p_hi[c][:, n, q], v_hi[:, n, :],
                                     start=(n == 0), stop=False)
                    nc.tensor.matmul(o_ps[t % 2][:, 0:D], p_hi[c][:, n, q], v_lo[:, n, :],
                                     start=False, stop=False)
                    mm = nc.tensor.matmul(o_ps[t % 2][:, 0:D + ONES], p_lo[c][:, n, q], v_hi[:, n, :],
                                          start=False, stop=(n == TILES - 1))
                mm.then_inc(pv_mm, 1)

            def batch(b, last):
                project_z(b)
                scores(b, 0)
                for n in range(TILES):
                    project_vf(b, n)
                scores(b, 1)
                for t in range(CT):
                    p_times_v(b, t)
                if not last:
                    transpose_x(b + 1)
                for t in range(CT, TILES):
                    p_times_v(b, t)

            pe.wait_ge(a_lo_made, 1)
            pe.wait_ge(wv_lo_made, 1)
            transpose_x(0)
            pe.wait_ge(ffn_lo_made, 1)
            pe.wait_ge(from_bias_made, 1)
            pe.wait_ge(ones_made, 1)
            batch(0, last=False)
            with pe.Fori(1, B - 1) as b:
                batch(b, last=False)
            batch(B - 1, last=True)


_INS = ["L0_attn_x", "L0_attn_wq", "L0_attn_bq", "L0_attn_wk", "L0_attn_bk", "L0_attn_wv", "L0_attn_bv",
        "L0_ffn_W", "L0_ffn_b", "L0_ffn_lora_down", "L0_ffn_lora_up", "L0_ffn_down_aux", "L0_ffn_up_aux"]


def kernel(**inputs):
    import numpy as _np
    import concourse.bacc as _bacc
    from concourse import mybir as _mybir
    from concourse.bass_utils import run_bass_kernel_spmd as _run

    nc = _bacc.Bacc("TRN2", target_bir_lowering=False, num_devices=1)
    arrays, args = {}, []
    for name in _INS:
        a = _np.ascontiguousarray(inputs[name])
        arrays[f"in_{name}"] = a
        args.append(nc.dram_tensor(f"in_{name}", a.shape, _mybir.dt.from_np(a.dtype), kind="ExternalInput").ap())
    shape = tuple(inputs["L0_attn_x"].shape)
    args.append(nc.dram_tensor("out_0", shape, _mybir.dt.float32, kind="ExternalOutput").ap())
    attention_plus_lora_ffn(nc, *args)
    r = _run(nc, [arrays], core_ids=[0])
    return r.results[0]["out_0"]
```

```python
import concourse.bass as bass
from concourse import mybir
from contextlib import ExitStack


def attention_plus_lora_ffn(
    nc: bass.Bass,
    x: bass.AP,
    wq: bass.AP,
    bq: bass.AP,
    wk: bass.AP,
    bk: bass.AP,
    wv: bass.AP,
    bv: bass.AP,
    ffn_w: bass.AP,
    ffn_b: bass.AP,
    lora_down: bass.AP,
    lora_up: bass.AP,
    down_aux: bass.AP,
    up_aux: bass.AP,
    out: bass.AP,
):
    f32 = mybir.dt.float32
    f32r = mybir.dt.float32r
    ALU = mybir.AluOpType
    ACT = mybir.ActivationFunctionType
    MAX = bass.bass_isa.ReduceOp.max

    B, S, D = x.shape
    PT = 128
    BANK = 512
    TILES = S // PT
    DT = D // PT
    CHUNKS = S // BANK
    CT = TILES // CHUNKS
    RING = 4
    ONES = 2
    BLOCKS = 8
    RANK, DDIM = lora_down.shape
    UDIM = lora_up.shape[0]
    SCALE = float(D) ** -0.5
    EPS = 1e-5
    DMA = 16

    x_v = x.rearrange("b (p n) d -> b p (n d)", n=TILES)
    out_v = out.rearrange("b (p n) d -> b p n d", n=TILES)

    def rows(w):
        return w.rearrange("(t p) n -> p t n", p=PT)

    def column(v):
        return v.rearrange("(t p) -> p t", p=PT)

    def row_for_all(v):
        return v.rearrange("(a n) -> a n", a=1).partition_broadcast(PT).rearrange("p a n -> p (a n)")

    ctx = ExitStack()
    with ctx:
        def sb(name, shape, dt=f32):
            return ctx.enter_context(nc.sbuf_tensor(name, shape, dt))

        def bank(name):
            return ctx.enter_context(nc.psum_tensor(name, [PT, BANK], f32))

        def sem(name):
            return ctx.enter_context(nc.semaphore(name))

        bq_col = sb("bq_col", [PT, DT])
        bk_col = sb("bk_col", [PT, DT])
        bias_all = sb("bias_all", [PT, D])
        lora_down_t = sb("lora_down_t", [DDIM, RANK])
        lora_up_t = sb("lora_up_t", [RANK, UDIM])
        identity = sb("identity", [PT, PT])
        minus_half = sb("minus_half", [PT, TILES])
        eps_all = sb("eps_all", [PT, TILES])
        a_hi = sb("a_hi", [PT, DT, D], f32r)
        a_lo = sb("a_lo", [PT, DT, D], f32r)
        vf_hi = sb("vf_hi", [PT, DT, 2 * D], f32r)
        vf_lo = sb("vf_lo", [PT, DT, 2 * D], f32r)
        e_row = sb("e_row", [PT, D])[:, :]
        b_parts = sb("b_parts", [PT, DT + 1])
        z_bias = b_parts[:, 0:DT]
        e_const = b_parts[:, DT:DT + 1]

        x_sb = sb("x_sb", [PT, TILES, D])
        xn = sb("xn", [PT, TILES, D])
        x_bias = sb("x_bias", [PT, TILES, D])
        prod = sb("prod", [PT, TILES, D])
        base = sb("base", [PT, TILES, D])
        stats = sb("stats", [PT, TILES, 6])
        mean_var = sb("mean_var", [PT, TILES, 2])
        var_eps = sb("var_eps", [PT, TILES])
        rstd = sb("rstd", [PT, TILES])
        e_sum = sb("e_sum", [PT, TILES])
        e = sb("e", [PT, TILES])
        xt_hi = sb("xt_hi", [PT, DT, S], f32r)
        xt_lo = sb("xt_lo", [PT, DT, S], f32r)
        zt_hi = sb("zt_hi", [PT, DT, S], f32r)
        zt_lo = sb("zt_lo", [PT, DT, S], f32r)
        v_hi = sb("v_hi", [PT, TILES, D + ONES], f32r)
        v_lo = sb("v_lo", [PT, TILES, D], f32r)
        p_sum_inv = sb("p_sum_inv", [PT, TILES])
        s = [sb(f"s{c}", [PT, TILES, BANK]) for c in range(CHUNKS)]
        p_hi = [sb(f"p_hi{c}", [PT, TILES, BANK], f32r) for c in range(CHUNKS)]
        p_lo = [sb(f"p_lo{c}", [PT, TILES, BANK], f32r) for c in range(CHUNKS)]
        down_aux_sb = s[0][0:DDIM, 0, 0:D]
        up_aux_pad = s[0][:, 0, D:2 * D].rearrange("p (t n) -> p t n", t=DT)
        low_rank = s[0][0:RANK, 1, 0:D]
        mid_rank = s[0][0:UDIM, 1, D:2 * D]
        early = s[CHUNKS - 1]
        wk_sb, wq_sb, wv_sb, ffn_w_sb = (
            early[:, i, :].rearrange("p (t n) -> p t n", t=DT) for i in range(4))
        wk_hi, wk_lo, wq_hi, wq_lo = (
            p_hi[0][:, i, :].rearrange("p (t n) -> p t n", t=DT) for i in range(4))
        bv_all, ffn_b_all = (early[:, 4, i * D:(i + 1) * D] for i in range(2))
        up_aux_t = early[:, 5, 0:D]
        bq_wide = early[:, 5, D:2 * D].rearrange("p (t n) -> p t n", t=DT)
        tile_max = [sb(f"tile_max{c}", [PT, BANK]) for c in range(CHUNKS)]
        top = [sb(f"top{c}", [PT, BANK]) for c in range(CHUNKS)]

        gate = sb("gate", [PT, 1])

        s_ps = [bank(f"s_ps{i}") for i in range(RING)]
        o_ps = [bank(f"o_ps{i}") for i in range(2)]
        g_ps = [bank(f"g_ps{i}") for i in range(2)]

        x0_loaded = [sem(f"x0_loaded{j}") for j in range(4)]
        x_loaded = sem("x_loaded")
        wk_loaded = sem("wk_loaded")
        wq_loaded = sem("wq_loaded")
        b_qk_loaded = sem("b_qk_loaded")
        lora_loaded = sem("lora_loaded")
        vw_loaded = sem("vw_loaded")
        bias_loaded = sem("bias_loaded")
        stored = [sem(f"stored{j}") for j in range(TILES // 2)]
        last_stored = [sem(f"last_stored{i}") for i in range(2)]
        zeroed = sem("zeroed")
        ones_made = sem("ones_made")
        identity_made = sem("identity_made")
        bq_spread = sem("bq_spread")
        bias_made = sem("bias_made")
        a_mm = sem("a_mm")
        e_row_mm = sem("e_row_mm")
        b_parts_mm = sem("b_parts_mm")
        low_rank_mm = sem("low_rank_mm")
        up_aux_t_mm = sem("up_aux_t_mm")
        mid_rank_mm = sem("mid_rank_mm")
        wv_t_mm = sem("wv_t_mm")
        ffn_t_mm = sem("ffn_t_mm")
        wk_hi_made = sem("wk_hi_made")
        wk_lo_made = sem("wk_lo_made")
        wq_hi_made = sem("wq_hi_made")
        wq_lo_made = sem("wq_lo_made")
        a_hi_made = sem("a_hi_made")
        a_lo_made = sem("a_lo_made")
        e_row_made = sem("e_row_made")
        b_parts_made = sem("b_parts_made")
        wv_hi_made = sem("wv_hi_made")
        wv_lo_made = sem("wv_lo_made")
        low_rank_made = sem("low_rank_made")
        up_aux_t_made = sem("up_aux_t_made")
        mid_rank_made = sem("mid_rank_made")
        ffn_hi_made = sem("ffn_hi_made")
        ffn_lo_made = sem("ffn_lo_made")
        stats_made = sem("stats_made")
        mean_var_made = sem("mean_var_made")
        var_eps_made = sem("var_eps_made")
        rstd_made = sem("rstd_made")
        xn_made = sem("xn_made")
        x_bias_made = sem("x_bias_made")
        prod_made = sem("prod_made")
        e_sum_made = sem("e_sum_made")
        e_made = sem("e_made")
        xt_mm = sem("xt_mm")
        xt_hi_made = sem("xt_hi_made")
        xt_lo_made = sem("xt_lo_made")
        zt_mm = sem("zt_mm")
        zt_hi_made = sem("zt_hi_made")
        zt_lo_made = sem("zt_lo_made")
        vf_mm = sem("vf_mm")
        v_hi_made = sem("v_hi_made")
        v_lo_made = sem("v_lo_made")
        base_made = sem("base_made")
        score_mm = sem("score_mm")
        tile_max_made = sem("tile_max_made")
        s_made = sem("s_made")
        gate_made = sem("gate_made")
        top_made = sem("top_made")
        shifted = sem("shifted")
        p_made = sem("p_made")
        p_hi_made = sem("p_hi_made")
        p_lo_made = sem("p_lo_made")
        pv_mm = sem("pv_mm")
        inv_made = sem("inv_made")
        out_made = sem("out_made")

        def wait(eng, semaphore, count):
            if isinstance(count, int) and count <= 0:
                return
            eng.wait_ge(semaphore, count)

        GROUPS = [(h, d) for h in range(2) for d in range(DT)]
        NG = len(GROUPS)
        xt_bank = [g_ps[0], g_ps[1], s_ps[0], s_ps[1]]
        zt_bank = [g_ps[0], g_ps[1], s_ps[2], s_ps[3]]
        vf_bank = [g_ps[0], g_ps[1], o_ps[0], o_ps[1]]
        NV = len(vf_bank)
        HT = TILES // 2

        def half(h):
            return slice(h * (S // 2), (h + 1) * (S // 2))

        def two(ap):
            return ap.rearrange("p (t n) -> p t n", t=DT)

        HQ = BANK // 2
        PAIRS = TILES // 2

        def block_of(j):
            h, pair = divmod(j, PAIRS)
            return slice(2 * pair, 2 * pair + 2), slice(h * HQ, (h + 1) * HQ)

        block = ctx.enter_context(nc.Block())

        @block.sync
        def _(sp):
            for j in range(4):
                n = TILES // 4
                sp.dma_start(x_sb[:, j * n:(j + 1) * n, :],
                             x_v[0, :, j * n * D:(j + 1) * n * D].rearrange("p (n d) -> p n d", d=D))\
                  .then_inc(x0_loaded[j], DMA)
            sp.dma_start(wk_sb[:, :, :], rows(wk)).then_inc(wk_loaded, DMA)
            sp.dma_start(wq_sb[:, :, :], rows(wq)).then_inc(wq_loaded, DMA)
            sp.dma_start(wv_sb[:, :, :], rows(wv)).then_inc(vw_loaded, DMA)
            sp.dma_start(ffn_w_sb[:, :, :], rows(ffn_w)).then_inc(vw_loaded, DMA)
            sp.dma_start(bv_all[:, :], row_for_all(bv)).then_inc(bias_loaded, DMA)
            sp.dma_start(ffn_b_all[:, :], row_for_all(ffn_b)).then_inc(bias_loaded, DMA)

            def load(b):
                sp.wait_ge(xn_made, TILES * b)
                sp.wait_ge(x_bias_made, b)
                sp.dma_start(x_sb[:, :, :], x_v[b, :, :].rearrange("p (n d) -> p n d", d=D))\
                  .then_inc(x_loaded, DMA)

            def store(b, j):
                sp.wait_ge(out_made, TILES * b + 2 * j + 2)
                sp.dma_start(out_v[b, :, 2 * j:2 * j + 2, :], base[:, 2 * j:2 * j + 2, :])\
                  .then_inc(stored[j], DMA)

            load(1)
            with sp.Fori(0, B - 2) as b:
                for j in range(CT // 2):
                    store(b, j)
                load(b + 2)
                for j in range(CT // 2, TILES // 2):
                    store(b, j)
            for b in range(B - 2, B):
                for j in range(TILES // 2 - (b == B - 1)):
                    store(b, j)
            for t in range(TILES - 2, TILES):
                sp.wait_ge(out_made, TILES * (B - 1) + t + 1)
                sp.dma_start(out_v[B - 1, :, t, :], base[:, t, :]).then_inc(last_stored[t % 2], DMA)
            for j in range(TILES // 2):
                sp.wait_ge(stored[j], DMA * (B - (j == TILES // 2 - 1)))
            for tile_stored in last_stored:
                sp.wait_ge(tile_stored, DMA)

        @block.gpsimd
        def _(pool):
            nc.gpsimd.memset(identity[:, :], 0.0).then_inc(zeroed, 1)
            nc.gpsimd.memset(up_aux_pad[:, :, :], 0.0).then_inc(zeroed, 1)
            nc.gpsimd.memset(minus_half[:, :], -0.5).then_inc(zeroed, 1)
            nc.gpsimd.memset(eps_all[:, :], EPS).then_inc(zeroed, 1)
            pool.wait_ge(zeroed, 1)
            nc.gpsimd.affine_select(out=identity[:, :], in_=identity[:, :], compare_op=ALU.not_equal, fill=1.0,
                                    base=0, pattern=[[-1, PT]], channel_multiplier=1).then_inc(identity_made, 1)
            nc.gpsimd.memset(v_hi[:, :, D:D + ONES].bitcast(f32), 1.0).then_inc(ones_made, 1)
            pool.wait_ge(zeroed, 4)

            def make_rstd(b):
                pool.wait_ge(mean_var_made, TILES * (b + 1))
                nc.gpsimd.tensor_tensor(var_eps[:, :], mean_var[:, :, 1], eps_all[:, :], ALU.add)\
                  .then_inc(var_eps_made, 1)
                pool.wait_ge(var_eps_made, b + 1)
                nc.gpsimd.tensor_tensor(rstd[:, :], var_eps[:, :], minus_half[:, :], ALU.pow)\
                  .then_inc(rstd_made, 1)

            def make_x_bias(b):
                wait(pool, base_made, TILES * b)
                nc.gpsimd.tensor_tensor(x_bias[:, :, :], x_sb[:, :, :],
                                        bias_all[:, :].unsqueeze(1).to_broadcast([PT, TILES, D]), ALU.add)\
                  .then_inc(x_bias_made, 1)

            def make_prod(b):
                wait(pool, e_sum_made, TILES * b)
                for i in range(TILES // 2):
                    pool.wait_ge(xn_made, TILES * b + 2 * i + 2)
                    nc.gpsimd.tensor_tensor(prod[:, 2 * i:2 * i + 2, :], xn[:, 2 * i:2 * i + 2, :],
                                            e_row.unsqueeze(1).to_broadcast([PT, 2, D]), ALU.mult)\
                      .then_inc(prod_made, 1)

            def make_top(b, c):
                wait(pool, gate_made, CHUNKS * b + c)
                pool.wait_ge(tile_max_made, TILES * (CHUNKS * b + c + 1))
                nc.gpsimd.tensor_tensor(gate[:, :], tile_max[c][:, 0:1], tile_max[c][:, 0:1], ALU.add)\
                  .then_inc(gate_made, 1)
                for h in range(2):
                    q = slice(h * HQ, (h + 1) * HQ)
                    nc.gpsimd.partition_all_reduce(top[c][:, q], tile_max[c][:, q], PT, MAX).then_inc(top_made, 1)

            def batch(b, last):
                if not last:
                    pool.wait_ge(x_loaded, DMA * (b + 1))
                    make_rstd(b + 1)
                make_top(b, 0)
                if not last:
                    make_prod(b + 1)
                make_top(b, 1)
                if not last:
                    make_x_bias(b + 1)

            for j in range(4):
                pool.wait_ge(x0_loaded[j], DMA)
            make_rstd(0)
            pool.wait_ge(e_row_made, 1)
            make_prod(0)
            pool.wait_ge(bias_loaded, 2 * DMA)
            nc.gpsimd.tensor_tensor(bias_all[:, :], bv_all[:, :], ffn_b_all[:, :], ALU.add).then_inc(bias_made, 1)
            pool.wait_ge(bias_made, 1)
            make_x_bias(0)
            batch(0, last=False)
            with pool.Fori(1, B - 1) as b:
                batch(b, last=False)
            batch(B - 1, last=True)

        @block.scalar
        def _(act):
            with nc.allow_non_contiguous_dma(reason="a few hundred words of biases and LoRA factors"):
                act.dma_start(bq_col[:, :], column(bq)).then_inc(b_qk_loaded, DMA)
                act.dma_start(bk_col[:, :], column(bk)).then_inc(b_qk_loaded, DMA)
                act.dma_start(lora_down_t[:, :], lora_down.rearrange("r d -> d r")).then_inc(lora_loaded, DMA)
                act.dma_start(lora_up_t[:, :], lora_up.rearrange("u r -> r u")).then_inc(lora_loaded, DMA)
            act.dma_start(down_aux_sb[:, :], down_aux).then_inc(lora_loaded, DMA)
            act.wait_ge(zeroed, 2)
            act.dma_start(up_aux_pad[:, :, 0:UDIM], rows(up_aux)).then_inc(lora_loaded, DMA)

            act.wait_ge(wk_loaded, DMA)
            nc.scalar.activation(wk_hi, wk_sb, ACT.Copy).then_inc(wk_hi_made, 1)
            act.wait_ge(wq_loaded, DMA)
            nc.scalar.activation(wq_hi, wq_sb, ACT.Copy).then_inc(wq_hi_made, 1)
            act.wait_ge(low_rank_mm, 1)
            nc.scalar.activation(low_rank[:, :], o_ps[0][0:RANK, 0:D], ACT.Copy).then_inc(low_rank_made, 1)
            act.wait_ge(a_mm, 1)
            nc.scalar.activation(a_hi[:, :, :], two(s_ps[2][:, :]), ACT.Copy, scale=SCALE).then_inc(a_hi_made, 1)

            def make_xt_hi(b):
                for g, (h, d) in enumerate(GROUPS):
                    act.wait_ge(xt_mm, NG * b + g + 1)
                    nc.scalar.activation(xt_hi[:, d, half(h)], xt_bank[g][:, :], ACT.Copy).then_inc(xt_hi_made, 1)

            def make_e_sum(b, tiles):
                for n in tiles:
                    if n % 2 == 0:
                        act.wait_ge(prod_made, TILES // 2 * b + n // 2 + 1)
                    nc.scalar.activation(prod[:, n, :], prod[:, n, :], ACT.Copy,
                                         accum_out=e_sum[:, n:n + 1]).then_inc(e_sum_made, 1)

            def make_e(b):
                act.wait_ge(e_sum_made, TILES * (b + 1))
                nc.scalar.activation(e[:, :], e_sum[:, :], ACT.Identity, bias=e_const).then_inc(e_made, 1)

            def make_zt_hi(b, groups):
                for g in groups:
                    h, d = GROUPS[g]
                    act.wait_ge(zt_mm, NG * b + g + 1)
                    nc.scalar.activation(zt_hi[:, d, half(h)], zt_bank[g][:, :], ACT.Identity,
                                         bias=z_bias[:, d:d + 1]).then_inc(zt_hi_made, 1)

            def make_v_hi(b, n):
                act.wait_ge(vf_mm, TILES * b + n + 1)
                nc.scalar.activation(v_hi[:, n, 0:D], vf_bank[n % NV][:, 0:D], ACT.Copy).then_inc(v_hi_made, 1)

            def make_s(b, c, n):
                act.wait_ge(tile_max_made, TILES * (CHUNKS * b + c) + n + 1)
                nc.scalar.activation(s[c][:, n, :], s_ps[n % RING][:, :], ACT.Identity, bias=e[:, n:n + 1])\
                  .then_inc(s_made, 1)

            def make_p(b, c, j):
                keys, q = block_of(j)
                act.wait_ge(shifted, BLOCKS * (CHUNKS * b + c) + j + 1)
                nc.scalar.activation(s[c][:, keys, q], s[c][:, keys, q], ACT.Exp).then_inc(p_made, 1)

            def make_p_hi(b, c, j):
                keys, q = block_of(j)
                act.wait_ge(p_made, BLOCKS * (CHUNKS * b + c) + j + 1)
                nc.scalar.activation(p_hi[c][:, keys, q], s[c][:, keys, q], ACT.Copy).then_inc(p_hi_made, 1)

            def batch(b, last):
                for n in range(TILES):
                    make_s(b, 0, n)
                for n in range(TILES):
                    make_v_hi(b, n)
                    if n >= 4:
                        make_p(b, 0, n - 4)
                    if n >= 5:
                        make_p_hi(b, 0, n - 5)
                make_p_hi(b, 0, 3)
                for n in range(TILES):
                    make_s(b, 1, n)
                    if 1 <= n <= PAIRS:
                        make_p(b, 0, PAIRS + n - 1)
                    elif n > PAIRS:
                        make_p_hi(b, 0, n - 1)
                make_p_hi(b, 0, BLOCKS - 1)
                for j in range(BLOCKS):
                    make_p(b, 1, j)
                    if j % PAIRS > 0:
                        make_p_hi(b, 1, j - 1)
                    if j % PAIRS == PAIRS - 1:
                        make_p_hi(b, 1, j)
                if not last:
                    make_xt_hi(b + 1)
                    make_e_sum(b + 1, range(TILES))
                    make_e(b + 1)
                    make_zt_hi(b + 1, range(NG))

            make_xt_hi(0)
            act.wait_ge(up_aux_t_mm, 1)
            nc.scalar.activation(up_aux_t[:, :], o_ps[1][:, 0:D], ACT.Copy).then_inc(up_aux_t_made, 1)
            act.wait_ge(mid_rank_mm, 1)
            nc.scalar.activation(mid_rank[:, :], o_ps[0][0:UDIM, D:2 * D], ACT.Copy).then_inc(mid_rank_made, 1)
            act.wait_ge(e_row_made, 1)
            act.wait_ge(b_parts_made, 1)
            for g in range(NG):
                make_e_sum(0, range(g * TILES // NG, (g + 1) * TILES // NG))
                make_zt_hi(0, [g])
            make_e(0)
            act.wait_ge(wv_t_mm, 1)
            nc.scalar.activation(vf_hi[:, :, 0:D], two(o_ps[0][:, :]), ACT.Copy).then_inc(wv_hi_made, 1)
            act.wait_ge(ffn_t_mm, 1)
            nc.scalar.activation(vf_hi[:, :, D:2 * D], two(o_ps[1][:, :]), ACT.Copy).then_inc(ffn_hi_made, 1)
            batch(0, last=False)
            with act.Fori(1, B - 1) as b:
                batch(b, last=False)
            batch(B - 1, last=True)

        @block.vector
        def _(dve):
            dve.wait_ge(b_qk_loaded, 2 * DMA)
            for o in range(DT):
                nc.vector.tensor_copy(bq_wide[:, o, :], bq_col[:, o:o + 1].to_broadcast([PT, PT]))\
                  .then_inc(bq_spread, 1)

            def make_stats(b, tiles):
                for n in tiles:
                    nc.vector.bn_stats(stats[:, n, :], x_sb[:, n, :]).then_inc(stats_made, 1)

            def make_mean_var(b):
                for n in range(TILES):
                    nc.vector.bn_aggr(mean_var[:, n, :], stats[:, n, :]).then_inc(mean_var_made, 1)

            def make_xn(b, tiles):
                dve.wait_ge(rstd_made, b + 1)
                wait(dve, xt_mm, NG * b)
                wait(dve, prod_made, TILES // 2 * b)
                for n in tiles:
                    nc.vector.tensor_scalar(xn[:, n, :], x_sb[:, n, :], mean_var[:, n, 0:1], rstd[:, n:n + 1],
                                            ALU.subtract, ALU.mult).then_inc(xn_made, 1)

            def make_xt_lo(b, groups):
                for g in groups:
                    h, d = GROUPS[g]
                    dve.wait_ge(xt_hi_made, NG * b + g + 1)
                    nc.vector.tensor_tensor(xt_lo[:, d, half(h)], xt_bank[g][:, :],
                                            xt_hi[:, d, half(h)].bitcast(f32), ALU.subtract).then_inc(xt_lo_made, 1)

            for j in range(4):
                dve.wait_ge(x0_loaded[j], DMA)
                make_stats(0, range(j * TILES // 4, (j + 1) * TILES // 4))
            dve.wait_ge(stats_made, TILES)
            make_mean_var(0)

            dve.wait_ge(wk_hi_made, 1)
            nc.vector.tensor_tensor(wk_lo, wk_sb, wk_hi.bitcast(f32), ALU.subtract).then_inc(wk_lo_made, 1)
            dve.wait_ge(wq_hi_made, 1)
            nc.vector.tensor_tensor(wq_lo, wq_sb, wq_hi.bitcast(f32), ALU.subtract).then_inc(wq_lo_made, 1)
            dve.wait_ge(e_row_mm, 1)
            nc.vector.tensor_scalar(e_row, s_ps[3][:, 0:D], SCALE, None, ALU.mult)\
              .then_inc(e_row_made, 1)
            make_xn(0, range(TILES))
            dve.wait_ge(a_hi_made, 1)
            nc.vector.scalar_tensor_tensor(a_lo[:, :, :].rearrange("p t n -> p (t n)"), s_ps[2][:, :], SCALE,
                                           a_hi[:, :, :].rearrange("p t n -> p (t n)").bitcast(f32),
                                           ALU.mult, ALU.subtract).then_inc(a_lo_made, 1)
            make_xt_lo(0, range(0, NG // 2))
            dve.wait_ge(b_parts_mm, 1)
            nc.vector.tensor_scalar(b_parts[:, :], s_ps[3][:, 0:DT + 1], SCALE, None, ALU.mult)\
              .then_inc(b_parts_made, 1)
            make_xt_lo(0, range(NG // 2, NG))
            def make_zt_lo(b):
                for g, (h, d) in enumerate(GROUPS):
                    dve.wait_ge(zt_hi_made, NG * b + g + 1)
                    nc.vector.scalar_tensor_tensor(zt_lo[:, d, half(h)], zt_bank[g][:, :], z_bias[:, d:d + 1],
                                                   zt_hi[:, d, half(h)].bitcast(f32), ALU.add, ALU.subtract)\
                      .then_inc(zt_lo_made, 1)

            def make_v_lo_and_base(b, n):
                dve.wait_ge(v_hi_made, TILES * b + n + 1)
                nc.vector.tensor_tensor(v_lo[:, n, :], vf_bank[n % NV][:, 0:D], v_hi[:, n, 0:D].bitcast(f32),
                                        ALU.subtract).then_inc(v_lo_made, 1)
                if n == 0:
                    dve.wait_ge(x_bias_made, b + 1)
                wait(dve, stored[n // 2], DMA * b)
                nc.vector.tensor_tensor(base[:, n, :], vf_bank[n % NV][:, D:2 * D], x_bias[:, n, :], ALU.add)\
                  .then_inc(base_made, 1)

            def make_tile_max(b, c, n):
                i = TILES * (CHUNKS * b + c) + n
                if n == 0:
                    dve.wait_ge(e_made, b + 1)
                    dve.wait_ge(score_mm, i + 1)
                    nc.vector.tensor_scalar(tile_max[c][:, :], s_ps[0][:, :], e[:, 0:1], None, ALU.add)\
                      .then_inc(tile_max_made, 1)
                else:
                    dve.wait_ge(tile_max_made, i)
                    dve.wait_ge(score_mm, i + 1)
                    nc.vector.scalar_tensor_tensor(tile_max[c][:, :], s_ps[n % RING][:, :], e[:, n:n + 1],
                                                   tile_max[c][:, :], ALU.add, ALU.max).then_inc(tile_max_made, 1)

            def shift(b, c, j):
                keys, q = block_of(j)
                dve.wait_ge(s_made, TILES * (CHUNKS * b + c) + keys.stop)
                if j % PAIRS == 0:
                    dve.wait_ge(top_made, 2 * (CHUNKS * b + c) + j // PAIRS + 1)
                nc.vector.tensor_tensor(s[c][:, keys, q], s[c][:, keys, q],
                                        top[c][:, q].unsqueeze(1).to_broadcast([PT, 2, HQ]), ALU.subtract)\
                  .then_inc(shifted, 1)

            def make_p_lo(b, c, j):
                keys, q = block_of(j)
                dve.wait_ge(p_hi_made, BLOCKS * (CHUNKS * b + c) + j + 1)
                nc.vector.tensor_tensor(p_lo[c][:, keys, q], s[c][:, keys, q], p_hi[c][:, keys, q].bitcast(f32),
                                        ALU.subtract).then_inc(p_lo_made, 1)

            def make_out(b, t):
                dve.wait_ge(pv_mm, TILES * b + t + 1)
                nc.vector.reciprocal(p_sum_inv[:, t:t + 1], o_ps[t % 2][:, D:D + 1]).then_inc(inv_made, 1)
                dve.wait_ge(inv_made, TILES * b + t + 1)
                nc.vector.scalar_tensor_tensor(base[:, t, :], o_ps[t % 2][:, 0:D], p_sum_inv[:, t:t + 1],
                                               base[:, t, :], ALU.mult, ALU.add).then_inc(out_made, 1)

            def batch(b, last):
                for n in range(TILES):
                    if n == 4 and not last:
                        dve.wait_ge(stats_made, TILES * (b + 2))
                    make_tile_max(b, 0, n)
                    if last:
                        continue
                    if n == 0:
                        dve.wait_ge(x_loaded, DMA * (b + 1))
                    if n < 4:
                        make_stats(b + 1, range(2 * n, 2 * n + 2))
                    elif n == 4:
                        make_mean_var(b + 1)
                    elif n == 6:
                        make_xn(b + 1, range(0, 2))
                for n in range(TILES):
                    make_v_lo_and_base(b, n)
                    if n < 3 and not last:
                        make_xn(b + 1, range(2 * n + 2, 2 * n + 4))
                    if 3 <= n < 7:
                        shift(b, 0, n - 3)
                make_p_lo(b, 0, 0)
                for n in range(TILES):
                    make_tile_max(b, 1, n)
                    if n < 4:
                        shift(b, 0, PAIRS + n)
                    elif n < 7:
                        make_p_lo(b, 0, n - 3)
                for j in range(PAIRS, BLOCKS - 1):
                    make_p_lo(b, 0, j)
                make_out(b, 0)
                shift(b, 1, 0)
                make_p_lo(b, 0, BLOCKS - 1)
                shift(b, 1, 1)
                make_out(b, 1)
                shift(b, 1, 2)
                shift(b, 1, 3)
                for i in range(PAIRS):
                    make_p_lo(b, 1, i)
                    if i == 1:
                        make_out(b, 2)
                    shift(b, 1, PAIRS + i)
                    if i == 2:
                        make_out(b, 3)
                make_p_lo(b, 1, PAIRS)
                make_p_lo(b, 1, PAIRS + 1)
                make_out(b, CT)
                make_p_lo(b, 1, PAIRS + 2)
                make_p_lo(b, 1, PAIRS + 3)
                if not last:
                    make_xt_lo(b + 1, range(0, NG // 2))
                make_out(b, CT + 1)
                if not last:
                    make_xt_lo(b + 1, range(NG // 2, NG))
                for t in range(CT + 2, TILES):
                    make_out(b, t)
                if not last:
                    make_zt_lo(b + 1)

            dve.wait_ge(b_parts_made, 1)
            make_zt_lo(0)
            dve.wait_ge(wv_hi_made, 1)
            nc.vector.tensor_tensor(vf_lo[:, :, 0:D], two(o_ps[0][:, :]), vf_hi[:, :, 0:D].bitcast(f32),
                                    ALU.subtract).then_inc(wv_lo_made, 1)
            dve.wait_ge(ffn_hi_made, 1)
            nc.vector.tensor_tensor(vf_lo[:, :, D:2 * D], two(o_ps[1][:, :]),
                                    vf_hi[:, :, D:2 * D].bitcast(f32), ALU.subtract).then_inc(ffn_lo_made, 1)
            batch(0, last=False)
            with dve.Fori(1, B - 1) as b:
                batch(b, last=False)
            batch(B - 1, last=True)

        @block.tensor
        def _(pe):
            def split_products(ps, left_hi, left_lo, right_hi, right_lo):
                for d in range(DT):
                    nc.tensor.matmul(ps, left_hi(d), right_hi(d), start=(d == 0), stop=False)
                    nc.tensor.matmul(ps, left_hi(d), right_lo(d), start=False, stop=False)
                    mm = nc.tensor.matmul(ps, left_lo(d), right_hi(d), start=False, stop=(d == DT - 1))
                return mm

            pe.wait_ge(bq_spread, DT)
            pe.wait_ge(wk_loaded, DMA)
            for o in range(DT):
                mm = nc.tensor.matmul(s_ps[3][:, 0:D], bq_wide[:, o, :], wk_sb[:, o, :],
                                 start=(o == 0), stop=(o == DT - 1))
            mm.then_inc(e_row_mm, 1)
            pe.wait_ge(lora_loaded, 4 * DMA)
            nc.tensor.matmul(o_ps[0][0:RANK, 0:D], lora_down_t[:, :], down_aux_sb[:, :],
                             start=True, stop=True).then_inc(low_rank_mm, 1)

            pe.wait_ge(wk_lo_made, 1)
            pe.wait_ge(wq_lo_made, 1)
            for d in range(DT):
                o_d = slice(d * PT, (d + 1) * PT)
                mm = split_products(s_ps[2][:, d * D:(d + 1) * D],
                                    lambda o: wk_hi[:, o, o_d], lambda o: wk_lo[:, o, o_d],
                                    lambda o: wq_hi[:, o, :], lambda o: wq_lo[:, o, :])
            mm.then_inc(a_mm, 1)

            def transpose_x(b):
                wait(pe, base_made, TILES * b)
                wait(pe, s_made, CHUNKS * TILES * b)
                for g, (h, d) in enumerate(GROUPS):
                    if d == 0:
                        pe.wait_ge(xn_made, TILES * b + (h + 1) * HT)
                    for n in range(HT):
                        mm = nc.tensor.transpose(xt_bank[g][:, n * PT:(n + 1) * PT],
                                                 xn[:, h * HT + n, d * PT:(d + 1) * PT], identity[:, :])
                    mm.then_inc(xt_mm, 1)

            def project_z(b):
                for g, (h, do) in enumerate(GROUPS):
                    if do == 0:
                        pe.wait_ge(xt_lo_made, NG * b + 2 * h + 2)
                    o = slice(do * PT, (do + 1) * PT)
                    split_products(zt_bank[g][:, :],
                                   lambda d: a_hi[:, d, o], lambda d: a_lo[:, d, o],
                                   lambda d: xt_hi[:, d, half(h)], lambda d: xt_lo[:, d, half(h)])\
                        .then_inc(zt_mm, 1)

            def project_vf(b, n):
                if n == 0:
                    pe.wait_ge(wv_lo_made, 1)
                    pe.wait_ge(ffn_lo_made, 1)
                    pe.wait_ge(ones_made, 1)
                if n == 2:
                    wait(pe, out_made, TILES * b)
                if n >= NV:
                    pe.wait_ge(base_made, TILES * b + n - NV + 1)
                t = slice(n * PT, (n + 1) * PT)
                split_products(vf_bank[n % NV][:, :],
                               lambda d: xt_hi[:, d, t], lambda d: xt_lo[:, d, t],
                               lambda d: vf_hi[:, d, :], lambda d: vf_lo[:, d, :]).then_inc(vf_mm, 1)

            def scores(b, c):
                q = slice(c * BANK, (c + 1) * BANK)
                for n in range(TILES):
                    wait(pe, s_made, TILES * (CHUNKS * b + c) + n - RING + 1)
                    if c == 0 and n in (0, 2, 3):
                        pe.wait_ge(zt_lo_made, NG * b + max(n, 1) + 1)
                    k = slice(n * PT, (n + 1) * PT)
                    split_products(s_ps[n % RING][:, :],
                                   lambda d: zt_hi[:, d, k], lambda d: zt_lo[:, d, k],
                                   lambda d: xt_hi[:, d, q], lambda d: xt_lo[:, d, q]).then_inc(score_mm, 1)

            def p_times_v(b, t):
                c, q = t // CT, slice(t % CT * PT, (t % CT + 1) * PT)
                if t == 0:
                    pe.wait_ge(v_lo_made, TILES * (b + 1))
                    pe.wait_ge(base_made, TILES * (b + 1))
                elif t >= 2:
                    pe.wait_ge(out_made, TILES * b + t - 1)
                for n in range(TILES):
                    if t % 2 == 0 and n % 2 == 0:
                        pe.wait_ge(p_lo_made, BLOCKS * (CHUNKS * b + c) + t % CT // 2 * PAIRS + n // 2 + 1)
                    nc.tensor.matmul(o_ps[t % 2][:, 0:D + ONES], p_hi[c][:, n, q], v_hi[:, n, :],
                                     start=(n == 0), stop=False)
                    nc.tensor.matmul(o_ps[t % 2][:, 0:D], p_hi[c][:, n, q], v_lo[:, n, :],
                                     start=False, stop=False)
                    mm = nc.tensor.matmul(o_ps[t % 2][:, 0:D + ONES], p_lo[c][:, n, q], v_hi[:, n, :],
                                          start=False, stop=(n == TILES - 1))
                mm.then_inc(pv_mm, 1)

            def batch(b, last):
                scores(b, 0)
                for n in range(TILES):
                    project_vf(b, n)
                scores(b, 1)
                for t in range(CT):
                    p_times_v(b, t)
                if not last:
                    transpose_x(b + 1)
                for t in range(CT, TILES):
                    p_times_v(b, t)
                if not last:
                    project_z(b + 1)

            transpose_x(0)
            pe.wait_ge(e_row_made, 1)
            pe.wait_ge(b_qk_loaded, 2 * DMA)
            for o in range(DT):
                nc.tensor.matmul(s_ps[3][:, DT:DT + 1], bq_wide[:, o, :], bk_col[:, o:o + 1],
                                      start=(o == 0), stop=(o == DT - 1))
            for d in range(DT):
                for o in range(DT):
                    mm = nc.tensor.matmul(s_ps[3][:, d:d + 1], wq_sb[:, o, d * PT:(d + 1) * PT],
                                          bk_col[:, o:o + 1], start=(o == 0), stop=(o == DT - 1))
            mm.then_inc(b_parts_mm, 1)
            pe.wait_ge(identity_made, 1)
            for o in range(DT):
                mm = nc.tensor.transpose(o_ps[1][:, o * PT:(o + 1) * PT], up_aux_pad[:, o, :], identity[:, :])
            mm.then_inc(up_aux_t_mm, 1)
            pe.wait_ge(low_rank_made, 1)
            nc.tensor.matmul(o_ps[0][0:UDIM, D:2 * D], lora_up_t[:, :], low_rank[:, :],
                             start=True, stop=True).then_inc(mid_rank_mm, 1)

            pe.wait_ge(a_lo_made, 1)
            pe.wait_ge(b_parts_made, 1)
            project_z(0)
            pe.wait_ge(vw_loaded, 2 * DMA)
            pe.wait_ge(mid_rank_made, 1)
            for d in range(DT):
                for o in range(DT):
                    mm = nc.tensor.transpose(o_ps[0][:, d * D + o * PT:d * D + (o + 1) * PT],
                                             wv_sb[:, o, d * PT:(d + 1) * PT], identity[:, :])
            mm.then_inc(wv_t_mm, 1)
            pe.wait_ge(up_aux_t_made, 1)
            for d in range(DT):
                for o in range(DT):
                    part = o_ps[1][:, d * D + o * PT:d * D + (o + 1) * PT]
                    nc.tensor.matmul(part, ffn_w_sb[:, o, d * PT:(d + 1) * PT], identity[:, :],
                                     start=True, stop=False)
                    mm = nc.tensor.matmul(part, mid_rank[:, d * PT:(d + 1) * PT],
                                          up_aux_t[0:UDIM, o * PT:(o + 1) * PT], start=False, stop=True)
            mm.then_inc(ffn_t_mm, 1)
            batch(0, last=False)
            with pe.Fori(1, B - 1) as b:
                batch(b, last=False)
            batch(B - 1, last=True)


_INS = ["L0_attn_x", "L0_attn_wq", "L0_attn_bq", "L0_attn_wk", "L0_attn_bk", "L0_attn_wv", "L0_attn_bv",
        "L0_ffn_W", "L0_ffn_b", "L0_ffn_lora_down", "L0_ffn_lora_up", "L0_ffn_down_aux", "L0_ffn_up_aux"]


def kernel(**inputs):
    import numpy as _np
    import concourse.bacc as _bacc
    from concourse import mybir as _mybir
    from concourse.bass_utils import run_bass_kernel_spmd as _run

    nc = _bacc.Bacc("TRN2", target_bir_lowering=False, num_devices=1)
    arrays, args = {}, []
    for name in _INS:
        a = _np.ascontiguousarray(inputs[name])
        arrays[f"in_{name}"] = a
        args.append(nc.dram_tensor(f"in_{name}", a.shape, _mybir.dt.from_np(a.dtype), kind="ExternalInput").ap())
    shape = tuple(inputs["L0_attn_x"].shape)
    args.append(nc.dram_tensor("out_0", shape, _mybir.dt.float32, kind="ExternalOutput").ap())
    attention_plus_lora_ffn(nc, *args)
    r = _run(nc, [arrays], core_ids=[0])
    return r.results[0]["out_0"]
```
